# Optimizing a Trainium2 kernel written in Bass

```python
import numpy as np
import jax
import jax.numpy as jnp

def _softmax(x, axis=-1):
    return jax.nn.softmax(x, axis=axis)

def _gelu(x):
    return jax.nn.gelu(x, approximate=True)

def _silu(x):
    return jax.nn.silu(x)

def _sigmoid(x):
    return jax.nn.sigmoid(x)

def _layernorm(x, axis=-1, eps=1e-05):
    m = jnp.mean(x, axis=axis, keepdims=True)
    v = jnp.var(x, axis=axis, keepdims=True)
    return (x - m) / jnp.sqrt(v + eps)

def _scatter_add(tgt, idx, src, axis=0):
    return tgt.at[idx].add(src)

def _segment_sum(src, seg, n):
    return jax.ops.segment_sum(src, seg, n)
kernel_name = 'mk_gnn_preln_d2_gnn_r8_0a64fb'

def setup_inputs(seed: int=0):
    np.random.seed(seed)
    _w = jnp.asarray

    def _rec_inputs():
        import jax
        import jax.numpy as jnp
        _gk = jax.random.key(seed)
        x = -0.0005121 + 1.001 * jax.random.normal(jax.random.fold_in(_gk, 1), (12500, 32), jnp.float32)
        _s = jax.random.randint(jax.random.fold_in(_gk, 2), (100000,), 0, 12500, jnp.int32)
        _d = jax.random.randint(jax.random.fold_in(_gk, 3), (100000,), 0, 12500, jnp.int32)
        _loop = jnp.arange(12500, dtype=jnp.int32)
        src = jnp.concatenate([_s, _d, _loop])
        dst = jnp.concatenate([_d, _s, _loop])
        _o = jnp.argsort(dst, stable=True)
        src = src[_o]
        dst = dst[_o]
        edge_attr_32 = 0.000216709 + 1.00012 * jax.random.normal(jax.random.fold_in(_gk, 12), (212500, 32), jnp.float32)
        edge_attr_4 = 0.000714719 + 1.00021 * jax.random.normal(jax.random.fold_in(_gk, 13), (212500, 4), jnp.float32)
        return (x, src, dst, edge_attr_32, edge_attr_4)
    x, src, dst, edge_attr_32, edge_attr_4 = _rec_inputs()

    def _L0_gnn_setup():
        import jax, jax.numpy as jnp
        import numpy as np
        N_NODES = 12500
        key = jax.random.key(seed)
        k1, k2, k3, k4 = jax.random.split(key, 4)
        features = jax.random.normal(k1, (N_NODES, 32), dtype=jnp.float32)
        src = jax.random.randint(k2, (200000,), 0, N_NODES, dtype=jnp.int64)
        dst = jax.random.randint(k3, (200000,), 0, N_NODES, dtype=jnp.int64)
        weight = jax.random.normal(k4, (32, 32), dtype=jnp.float32) * (1.0 / np.sqrt(32.0))
        bias = jnp.zeros((32,), dtype=jnp.float32)
        return {'features': features, 'src': src, 'dst': dst, 'weight': weight, 'bias': bias}
    _L0_gnn_all = _L0_gnn_setup()
    _L0_gnn_in = {k: v for k, v in _L0_gnn_all.items() if k in ('weight', 'bias')}
    del _L0_gnn_all

    def _L1_gnn_setup():
        import jax, jax.numpy as jnp
        import numpy as np
        MUL = 8
        N_NODES = 12500
        N_EDGES = 100000
        EDGE_DIM = 32
        MLP_DIM = 64
        W_NUMEL = 4 * MUL * MUL
        ALPHA = 0.25
        C110 = 1.0 / np.sqrt(3.0)
        SI_SCALE = 1.0 / np.sqrt(MUL)
        key = jax.random.key(seed)
        ks = jax.random.split(key, 10)
        node_attr = jax.random.normal(ks[0], (N_NODES, 4 * MUL), dtype=jnp.float32)
        edge_index = jax.random.randint(ks[1], (2, N_EDGES), 0, N_NODES, dtype=jnp.int64)
        edge_sh = jax.random.normal(ks[2], (N_EDGES, 4), dtype=jnp.float32)
        edge_feat = jax.random.normal(ks[3], (N_EDGES, EDGE_DIM), dtype=jnp.float32)
        W1 = jax.random.normal(ks[4], (EDGE_DIM, MLP_DIM), dtype=jnp.float32) / np.sqrt(EDGE_DIM)
        b1 = jnp.zeros((MLP_DIM,), dtype=jnp.float32)
        W2 = jax.random.normal(ks[5], (MLP_DIM, W_NUMEL), dtype=jnp.float32) / np.sqrt(MLP_DIM)
        b2 = jnp.zeros((W_NUMEL,), dtype=jnp.float32)
        si_w0 = jax.random.normal(ks[6], (MUL, MUL), dtype=jnp.float32)
        si_w1 = jax.random.normal(ks[7], (MUL, MUL), dtype=jnp.float32)
        return {'node_attr': node_attr, 'edge_index': edge_index, 'edge_sh': edge_sh, 'edge_feat': edge_feat, 'W1': W1, 'b1': b1, 'W2': W2, 'b2': b2, 'si_w0': si_w0, 'si_w1': si_w1}
    _L1_gnn_all = _L1_gnn_setup()
    _L1_gnn_in = {k: v for k, v in _L1_gnn_all.items() if k in ('W1', 'b1', 'W2', 'b2', 'si_w0', 'si_w1')}
    del _L1_gnn_all
    return {'x': x, 'src': src, 'dst': dst, 'edge_attr_32': edge_attr_32, 'edge_attr_4': edge_attr_4, 'L0_gnn_weight': _L0_gnn_in['weight'], 'L0_gnn_bias': _L0_gnn_in['bias'], 'L1_gnn_W1': _L1_gnn_in['W1'], 'L1_gnn_b1': _L1_gnn_in['b1'], 'L1_gnn_W2': _L1_gnn_in['W2'], 'L1_gnn_b2': _L1_gnn_in['b2'], 'L1_gnn_si_w0': _L1_gnn_in['si_w0'], 'L1_gnn_si_w1': _L1_gnn_in['si_w1']}

def reference(x, src, dst, edge_attr_32, edge_attr_4, L0_gnn_weight, L0_gnn_bias, L1_gnn_W1, L1_gnn_b1, L1_gnn_W2, L1_gnn_b2, L1_gnn_si_w0, L1_gnn_si_w1):
    import jax
    import jax.numpy as jnp

    def _L0_gnn_ref(features, src, dst, weight, bias):
        import jax, jax.numpy as jnp
        import numpy as np
        N_NODES = 12500
        n = features.shape[0]
        ones = jnp.ones(src.shape[0], dtype=features.dtype)
        deg_out = jax.ops.segment_sum(ones, src, num_segments=n)
        deg_in = jax.ops.segment_sum(ones, dst, num_segments=n)
        norm_src = jax.lax.rsqrt(jnp.maximum(deg_out, 1.0))
        norm_dst = jax.lax.rsqrt(jnp.maximum(deg_in, 1.0))
        h = features * norm_src[:, None]
        msgs = h[src]
        agg = jax.ops.segment_sum(msgs, dst, num_segments=n)
        agg = agg * norm_dst[:, None]
        out = agg @ weight + bias
        return jax.nn.relu(out)

    def _L1_gnn_ref(node_attr, edge_index, edge_sh, edge_feat, W1, b1, W2, b2, si_w0, si_w1):
        import jax, jax.numpy as jnp
        import numpy as np
        MUL = 8
        N_NODES = 12500
        N_EDGES = 100000
        EDGE_DIM = 32
        MLP_DIM = 64
        W_NUMEL = 4 * MUL * MUL
        ALPHA = 0.25
        C110 = 1.0 / np.sqrt(3.0)
        SI_SCALE = 1.0 / np.sqrt(MUL)
        n = node_attr.shape[0]
        e = edge_sh.shape[0]
        h = jax.nn.relu(edge_feat @ W1 + b1)
        w = (h @ W2 + b2).reshape(e, 4, MUL, MUL)
        w_000, w_011, w_101, w_110 = (w[:, 0], w[:, 1], w[:, 2], w[:, 3])
        s = node_attr[:, :MUL]
        v = node_attr[:, MUL:].reshape(n, MUL, 3)
        src, dst = (edge_index[0], edge_index[1])
        s_e = s[src]
        v_e = v[src]
        sh0 = edge_sh[:, 0]
        sh1 = edge_sh[:, 1:4]
        m0 = ALPHA * (jnp.einsum('ei,eio->eo', s_e * sh0[:, None], w_000) + C110 * jnp.einsum('eim,em,eio->eo', v_e, sh1, w_110))
        m1 = ALPHA * (jnp.einsum('ei,em,eio->eom', s_e, sh1, w_011) + jnp.einsum('eim,eio->eom', v_e * sh0[:, None, None], w_101))
        out0 = jax.ops.segment_sum(m0, dst, num_segments=n)
        out1 = jax.ops.segment_sum(m1.reshape(e, MUL * 3), dst, num_segments=n).reshape(n, MUL, 3)
        out0 = out0 + SI_SCALE * (s @ si_w0)
        out1 = out1 + SI_SCALE * jnp.einsum('nim,io->nom', v, si_w1)
        return jnp.concatenate([out0, out1.reshape(n, MUL * 3)], axis=-1)
    edge_index = jnp.stack([src, dst])
    h = jnp.maximum(_layernorm(x, axis=-1), 0.0)
    x = x + _L0_gnn_ref(h, src, dst, L0_gnn_weight, L0_gnn_bias)
    h = jnp.maximum(_layernorm(x, axis=-1), 0.0)
    x = x + _L1_gnn_ref(h, edge_index, edge_attr_4, edge_attr_32, L1_gnn_W1, L1_gnn_b1, L1_gnn_W2, L1_gnn_b2, L1_gnn_si_w0, L1_gnn_si_w1)
    return x

_drawn_inputs = setup_inputs


def setup_inputs(seed=0):
    import zlib

    import numpy as np

    out = dict(_drawn_inputs(seed))
    spreads = {'L0_gnn_bias': (0.0, 0.1), 'L1_gnn_b1': (0.0, 0.1), 'L1_gnn_b2': (0.0, 0.1)}
    factors = {}
    for name, (base, spread) in spreads.items():
        noise = np.random.default_rng([zlib.crc32(name.encode()), seed]).standard_normal(out[name].shape)
        drawn = base * np.exp(spread * noise) if base else spread * noise
        out[name] = jnp.asarray(drawn.astype(out[name].dtype))
    for name, factor in factors.items():
        out[name] = (out[name] * factor).astype(out[name].dtype)
    return out
```

```python
from contextlib import ExitStack

import numpy as np
import concourse.bass as bass
from concourse import mybir

ALU = mybir.AluOpType
ACT = mybir.ActivationFunctionType
F32 = mybir.dt.float32
BF16 = mybir.dt.bfloat16
I32 = mybir.dt.int32
AX = mybir.AxisListType.X

P = 128
N_NODES, N_EDGES = 12500, 212500
FEAT, HID, MUL = 32, 64, 8
NR = -(-N_NODES // P)
NODES = P * NR
TILES = 8
CHUNK = TILES * P
RING = 4
CHUNKS = -(-N_EDGES // (CHUNK * RING)) * RING
ITERS = CHUNKS // RING
WIN = 68
ACC_W = NODES + WIN
N_PARAMS = 8 + RING
EPS = 1e-5
ALPHA, C110, SI_SCALE = 0.25, 1.0 / np.sqrt(3.0), 1.0 / np.sqrt(float(MUL))
HB = 16
HBATCH = CHUNKS * TILES // HB
RNE = 12582912.0
MID_R = 15
FIN_R = 16
MW = 56


def gnn_program(nc, x_nodes, src_all, src_chunks, dst_all, dst_chunks, edge_t, sh_chunks,
                w_l0, b_l0, w1, b1, w2, skip_w, sel_a, sel_b, ident_in, out):
    assert CHUNKS % (2 * HB // TILES) == 0 and CHUNKS % 2 == 0
    with ExitStack() as ctx:
        def sb(name, shape, dt=F32):
            return ctx.enter_context(nc.sbuf_tensor(name, shape, dt))

        def sem(name):
            return ctx.enter_context(nc.semaphore(name))

        table1 = nc.dram_tensor("table1", [NODES, FEAT], F32).ap()
        table2 = nc.dram_tensor("table2", [NODES, FEAT], F32).ap()
        bounds = nc.dram_tensor("bounds", [2, CHUNKS], F32).ap()

        ps = ctx.enter_context(nc.psum_tensor("ps", [P, 8, 512], F32))
        W_BANK, H_BANK, S_BANK = 0, 4, 6

        acc_a = sb("acc_a", [P, ACC_W])
        acc_b = sb("acc_b", [P, ACC_W])
        x = sb("x", [P, NR, FEAT])
        xc = sb("xc", [P, NR, FEAT])
        hn = sb("hn", [P, NR, FEAT])
        stat = sb("stat", [P, 4, NR])
        norm_src = sb("norm_src", [P, NR])
        root = sb("root", [P, NR])
        dst_rel = sb("dst_rel", [P, CHUNKS * TILES])
        bound = sb("bound", [P, 2, CHUNKS])
        row_i = sb("row_i", [1, 2, CHUNKS], I32)
        dst_c = sb("dst_c", [CHUNKS // 2, 2, CHUNK], I32)
        mm_c = sb("mm_c", [CHUNKS // 2, 2, 2])
        iota_w = sb("iota_w", [P, WIN])
        idx = sb("idx", [P, RING, TILES], I32)
        g = sb("g", [P, RING, TILES, FEAT + 1])
        sh = sb("sh", [P, RING, TILES, 4])
        onehot = sb("onehot", [P, 2, TILES, WIN])
        onehot_x = sb("onehot_x", [P, TILES, WIN])
        dst_x = sb("dst_x", [P, TILES])
        ef = sb("ef", [P, CHUNK])
        hid = sb("hid", [P, 2, 512])
        q = sb("q", [P, 2, TILES, 48])
        vsh = sb("vsh", [P, TILES, MUL, 3])
        prod_a = sb("prod_a", [P, 2, TILES, 128])
        prod_b = sb("prod_b", [P, 2, 4, 4, 64])
        msg_b = sb("msg_b", [P, 2, TILES, MW])
        ident = sb("ident", [P, P])
        w_l0_s = sb("w_l0_s", [FEAT + 1, FEAT + 1])
        b_l0_s = sb("b_l0_s", [P, FEAT])
        w1_s = sb("w1_s", [P, HID])
        b1_s = sb("b1_s", [HID, 1])
        w2_s = sb("w2_s", [P, 4 * MUL * MUL])
        sel_a_s = sb("sel_a_s", [P, FEAT])
        sel_b_s = sb("sel_b_s", [96, FEAT])

        hist = acc_b[:, :].bitcast(BF16)
        T_ALL = CHUNKS * TILES
        o = 0
        dig_p, o = hist[:, o:o + T_ALL], o + T_ALL
        dig_r, o = hist[:, o:o + T_ALL], o + T_ALL
        iota_p, o = hist[:, o:o + P * HB].rearrange("p (j t) -> p j t", t=HB), o + P * HB
        iota_r, o = hist[:, o:o + NR * HB].rearrange("p (j t) -> p j t", t=HB), o + NR * HB
        oh_p, o = hist[:, o:o + 2 * P * HB].rearrange("p (b j t) -> p b j t", b=2, t=HB), o + 2 * P * HB
        oh_r, o = hist[:, o:o + 2 * NR * HB].rearrange("p (b j t) -> p b j t", b=2, t=HB), o + 2 * NR * HB
        zero_b, o = hist[:, o:o + P], o + P
        src_i = hn[:, :, :].rearrange("p r f -> p (r f)")[:, 0:T_ALL].bitcast(I32)
        src_f = xc[:, :, :].rearrange("p r f -> p (r f)")[:, 0:T_ALL]
        dst_i = acc_a[:, 0:T_ALL].bitcast(I32)

        src_loaded, dst_loaded, dstc_loaded, x_loaded, par_loaded = (
            sem(n) for n in ("src_loaded", "dst_loaded", "dstc_loaded", "x_loaded", "par_loaded"))
        bounds_done, bounds_out, bounds_in = sem("bounds_done"), sem("bounds_out"), sem("bounds_in")
        iota_done = sem("iota_done")
        hist_ready, hist_used, degrees_done = sem("hist_ready"), sem("hist_used"), sem("degrees_done")
        dve_chain = sem("dve_chain")
        params_clear = sem("params_clear")
        setup_done = sem("setup_done")
        table1_ready, table1_out = sem("table1_ready"), sem("table1_out")
        table2_ready, table2_out = sem("table2_ready"), sem("table2_out")
        idx_in = [sem(f"idx_in{j}") for j in range(RING)]
        sh_in = [sem(f"sh_in{j}") for j in range(RING)]
        ef_in = [sem(f"ef_in{j}") for j in range(RING)]
        gathered = [sem(f"gathered{j}") for j in range(RING)]
        onehot1_ready, seg1_done, added1 = sem("onehot1_ready"), sem("seg1_done"), sem("added1")
        mid_ready = sem("mid_ready")
        hidden_psum, hidden_ready = sem("hidden_psum"), sem("hidden_ready")
        weights_ready, weights_used = sem("weights_ready"), sem("weights_used")
        coefs_ready, vsh_ready, d_ready = sem("coefs_ready"), sem("vsh_ready"), sem("d_ready")
        prodb_ready, reduced, messages_ready = sem("prodb_ready"), sem("reduced"), sem("messages_ready")
        seg2_done, added2 = sem("seg2_done"), sem("added2")
        turned, turned_used = sem("turned"), sem("turned_used")
        acc_clear = sem("acc_clear")
        slots_opened = sem("slots_opened")
        root_asked, root_given = sem("root_asked"), sem("root_given")
        x_copied, x_shifted, x_onehot, x_seg, x_added = (
            sem(n) for n in ("x_copied", "x_shifted", "x_onehot", "x_seg", "x_added"))
        fin_ready, out_ready, out_stored = sem("fin_ready"), sem("out_ready"), sem("out_stored")

        def wait(eng, s, value):
            if not isinstance(value, int) or value > 0:
                eng.wait_ge(s, value)

        def over_iterations(eng, body):
            body(0)
            with eng.Fori(1, ITERS - 1) as i:
                body(i)
            body(ITERS - 1)

        GATH = 16 * TILES
        w_ps = [ps[:, W_BANK + 2 * b:W_BANK + 2 * b + 2, :].rearrange("p b (u w) -> p (b u) w", w=256)
                for b in range(2)]
        block = ctx.enter_context(nc.Block())

        @block.sync
        def _(sp):
            sp.dma_start(src_i, src_all).then_inc(src_loaded, 16)
            sp.dma_start(dst_c[:, :, :], dst_chunks.rearrange("(q s) e -> q s e", s=2)).then_inc(dstc_loaded, 16)
            sp.dma_start(dst_i, dst_all).then_inc(dst_loaded, 16)
            sp.dma_start(x[:, :, :], x_nodes.rearrange("p (r f) -> p r f", f=FEAT)).then_inc(x_loaded, 16)
            sp.dma_start(w_l0_s[:, :], w_l0).then_inc(par_loaded, 16)
            sp.dma_start(b_l0_s[:, :], b_l0.to_broadcast([P, FEAT])).then_inc(par_loaded, 16)
            for j in range(RING):
                sp.dma_start(w1_s[32 * j:32 * j + 32, :], w1).then_inc(par_loaded, 16)
            sp.dma_start(b1_s[:, :], b1).then_inc(par_loaded, 16)
            sp.wait_ge(params_clear, 1)
            sp.dma_start(w2_s[0:HID + 1, :], w2).then_inc(par_loaded, 16)
            sp.dma_start(sel_a_s[:, :], sel_a).then_inc(par_loaded, 16)
            sp.dma_start(sel_b_s[0:64, :], sel_b).then_inc(par_loaded, 16)
            sp.dma_start(sel_b_s[64:96, :], skip_w).then_inc(par_loaded, 16)
            sp.dma_start(ident[:, :], ident_in).then_inc(par_loaded, 16)
            sp.wait_ge(bounds_done, 2)
            for k in range(2):
                sp.dma_start(bounds[k:k + 1, :].rearrange("a (q s) -> (a q) s", s=2), mm_c[:, k, :]).then_inc(bounds_out, 16)
            sp.wait_ge(bounds_out, 32)
            for k in range(2):
                sp.dma_start(bound[:, k, :], bounds[k:k + 1, :].to_broadcast([P, CHUNKS])).then_inc(bounds_in, 16)

            for j in range(RING):
                sp.dma_start(idx[:, j, :], src_chunks[j]).then_inc(idx_in[j], 16)

            def load1(i):
                for j in range(RING):
                    sp.wait_ge(gathered[j], GATH * (i + 1))
                    sp.dma_start(idx[:, j, :], load_from(src_chunks, RING * i + RING + j)).then_inc(idx_in[j], 16)

            def load_from(dram, c):
                return dram[c] if isinstance(c, int) else dram[bass.ds(c, 1)].rearrange("a p k -> (a p) k")

            with sp.Fori(0, ITERS - 1) as i:
                load1(i)
            for j in range(RING):
                sp.dma_start(sh[:, j, :, :], sh_chunks[j].rearrange("p (t d) -> p t d", d=4)).then_inc(sh_in[j], 16)
                sp.dma_start(ef[32 * j:32 * j + 32, :], edge_t[j]).then_inc(ef_in[j], 16)
            for j in range(RING):
                sp.wait_ge(gathered[j], GATH * ITERS)
                sp.dma_start(idx[:, j, :], src_chunks[j]).then_inc(idx_in[j], 16)
            with sp.Fori(0, ITERS - 1) as i:
                for j in range(RING):
                    c = RING * i + j
                    sp.wait_ge(hidden_psum, 2 * c + 2)
                    sp.dma_start(ef[32 * j:32 * j + 32, :], load_from(edge_t, c + RING)).then_inc(ef_in[j], 16)
                    sp.wait_ge(gathered[j], GATH * (i + ITERS + 1))
                    sp.dma_start(idx[:, j, :], load_from(src_chunks, c + RING)).then_inc(idx_in[j], 16)
                    sp.wait_ge(messages_ready, c + 1)
                    sp.dma_start(sh[:, j, :, :].rearrange("p t d -> p (t d)"),
                                 load_from(sh_chunks, c + RING)).then_inc(sh_in[j], 16)
            for n in range(-(-NR // FIN_R)):
                sp.wait_ge(out_ready, n + 1)
                r0, r1 = n * FIN_R, min(NR, n * FIN_R + FIN_R)
                sp.dma_start(out.rearrange("(p r) f -> p r f", p=P)[:, r0:r1, :], xc[:, r0:r1, :]).then_inc(out_stored, 16)
            sp.wait_ge(out_stored, 16 * -(-NR // FIN_R))

        @block.gpsimd
        def _(pool):
            pool.iota(iota_p, [[1, P], [0, HB]], base=0, channel_multiplier=0,
                      allow_small_or_imprecise_dtypes=True).then_inc(iota_done, 1)
            pool.iota(iota_r, [[1, NR], [0, HB]], base=0, channel_multiplier=0,
                      allow_small_or_imprecise_dtypes=True).then_inc(iota_done, 1)
            pool.iota(iota_w[:, :], [[1, WIN]], base=0, channel_multiplier=0,
                      allow_small_or_imprecise_dtypes=True).then_inc(iota_done, 1)

            def gather(i, layer):
                table = (table1, table2)[layer]
                for j in range(RING):
                    pool.wait_ge(idx_in[j], 16 * (i + ITERS * layer + 1))
                    c = RING * i + j
                    if layer == 0:
                        wait(pool, onehot1_ready, c - 1 if not isinstance(c, int) or c >= RING else 0)
                    else:
                        wait(pool, d_ready, c - RING + 1)
                    pool.sem_inc(slots_opened, 1)
                    for t in range(TILES):
                        pool.indirect_dma_start(
                            out=g[:, j, t, 0:FEAT], out_offset=None, in_=table,
                            in_offset=bass.IndirectOffsetOnAxis(ap=idx[:, j, t:t + 1], axis=0),
                        ).then_inc(gathered[j], 16)

            pool.wait_ge(table1_out, 16)
            pool.wait_ge(setup_done, 1)
            over_iterations(pool, lambda i: gather(i, 0))
            pool.wait_ge(table2_out, 16)
            over_iterations(pool, lambda i: gather(i, 1))

        @block.scalar
        def _(act):
            def square_root(n):
                act.wait_ge(root_asked, n)
                act.activation(root[:, :], stat[:, 1, :], ACT.Sqrt).then_inc(root_given, 1)

            square_root(1)
            square_root(2)
            act.wait_ge(table1_ready, 1)
            act.dma_start(table1.rearrange("(p r) f -> p r f", p=P), hn[:, :, :]).then_inc(table1_out, 16)
            square_root(3)
            square_root(4)
            act.wait_ge(table2_ready, 1)
            act.dma_start(table2.rearrange("(p r) f -> p r f", p=P), hn[:, :, :]).then_inc(table2_out, 16)
            for n in range(-(-NR // 4)):
                k = min(4, NR - 4 * n)
                act.wait_ge(turned, n + 1)
                dest = acc_b[64:96, 0:NODES].rearrange("f (p r) -> f r p", r=NR)[:, 4 * n:4 * n + k, :]
                act.activation(dest, ps[0:32, S_BANK + n % 2, 0:128 * k].rearrange("f (r p) -> f r p", p=P),
                               ACT.Copy).then_inc(turned_used, 1)

            def relu(i, j, h):
                if isinstance(i, int) and i >= ITERS:
                    return
                act.wait_ge(hidden_psum, 2 * (RING * i + j) + h + 1)
                act.activation(hid[0:HID, h, :], ps[0:HID, H_BANK + h, :], ACT.Relu,
                               bias=b1_s[:, 0:1]).then_inc(hidden_ready, 1)

            def coefs(i, j):
                if isinstance(i, int) and i >= ITERS:
                    return
                c = RING * i + j
                act.wait_ge(gathered[j], GATH * (i + ITERS + 1))
                act.wait_ge(sh_in[j], 16 * (i + 1))
                wait(act, weights_used, 2 * c - 2)
                for t in range(TILES):
                    act.activation(q[:, j % 2, t, 8:40], g[:, j, t, 0:FEAT], ACT.Copy, scale=sh[:, j, t, 0:1])
                act.activation(q[:, j % 2, :, 40:48], g[:, j, :, 0:MUL], ACT.Copy).then_inc(coefs_ready, 1)

            def after(i, j, n):
                return i + (j + n) // RING, (j + n) % RING

            act.wait_ge(setup_done, 2)
            relu(0, 0, 0)
            relu(0, 0, 1)
            coefs(0, 0)
            relu(0, 1, 0)

            def steps(i):
                for j in range(RING):
                    relu(*after(i, j, 1), 1)
                    coefs(*after(i, j, 1))
                    relu(*after(i, j, 2), 0)

            over_iterations(act, steps)

        @block.tensor
        def _(pe):
            extra = pe.alloc_register("pe_extra")
            pe.reg_mov(extra, 0)

            deg = ps[:, H_BANK, 0:NR]
            pe.wait_ge(setup_done, 1)
            pe.matmul(deg, zero_b, zero_b[:, 0:NR], start=True, stop=False, skip_group_check=True)

            def count(i):
                for b in range(2):
                    pe.wait_ge(hist_ready, 2 * i + b + 1)
                    for t in range(HB):
                        mm = pe.matmul(deg, oh_p[:, b, :, t], oh_r[:, b, :, t], start=False, stop=False,
                                       skip_group_check=True)
                    mm.then_inc(hist_used, 1)

            with pe.Fori(0, HBATCH // 2) as i:
                count(i)
            pe.matmul(deg, zero_b, zero_b[:, 0:NR], start=False, stop=True,
                      skip_group_check=True).then_inc(degrees_done, 1)

            def segment_sums(oh, lhs, j, b, done, layer):
                groups = [(lhs[0], 0, 0)] if layer == 0 else [(lhs[0], 0, 0), (lhs[1], 128, 1)]
                for rows, col, _ in groups:
                    for t in range(TILES):
                        r = rows(t)
                        m = r.shape[1]
                        mm = pe.matmul(ps[0:m, S_BANK + b, col:col + WIN], r, oh(t),
                                       start=(t == 0), stop=(t == TILES - 1))
                mm.then_inc(done, 1)

            def more_windows(c, lhs, j, b, layer):
                span = pe.value_load(row_i[0:1, 1, bass.ds(c, 1)], min_val=0, max_val=NODES)
                with pe.If(span > WIN - 1):
                    with pe.Fori(WIN, span + 1, WIN):
                        pe.reg_add(extra, extra, 1)
                        pe.wait_ge(x_onehot, pe.snap(extra))
                        segment_sums(lambda t: onehot_x[:, t, :], lhs, j, b, x_seg, layer)

            def layer1(i):
                for j in range(RING):
                    c = RING * i + j
                    b = j % 2
                    lhs = [lambda t: g[:, j, t, :]]
                    pe.wait_ge(gathered[j], GATH * (i + 1))
                    pe.wait_ge(onehot1_ready, c + 1)
                    wait(pe, added1, c - 1)
                    segment_sums(lambda t: onehot[:, b, t, :], lhs, j, b, seg1_done, 0)
                    more_windows(c, lhs, j, b, 0)

            pe.wait_ge(setup_done, 2)
            over_iterations(pe, layer1)

            pe.wait_ge(par_loaded, 16 * N_PARAMS)
            pe.wait_ge(added1, CHUNKS + 1)
            acc_cols = acc_a[:, 0:NODES].rearrange("f (p r) -> f r p", r=NR)
            for n in range(-(-NR // MID_R)):
                r0, r1 = n * MID_R, min(NR, n * MID_R + MID_R)
                for r in range(r0, r1):
                    k = (r - r0) * (FEAT + 1)
                    mm = pe.matmul(ps[:, n, k:k + FEAT + 1], acc_cols[0:FEAT + 1, r, :], w_l0_s[:, :],
                                   start=True, stop=True)
                mm.then_inc(mid_ready, 1)

            pe.wait_ge(table2_ready, 1)
            for n in range(-(-NR // 4)):
                wait(pe, turned_used, n - 1)
                for r in range(4 * n, min(NR, 4 * n + 4)):
                    k = (r - 4 * n) * P
                    mm = pe.transpose(ps[0:32, S_BANK + n % 2, k:k + P], hn[:, r, :], ident[:, :])
                mm.then_inc(turned, 1)

            def half(i, j, ahead):
                j, h = j + ahead // 2, ahead % 2
                return i + j // RING, j % RING, h

            def beyond(i, j, h):
                return isinstance(i, int) and i >= ITERS

            def hidden(i, j, h):
                if beyond(i, j, h):
                    return
                k = 2 * (RING * i + j) + h
                if h == 0:
                    pe.wait_ge(ef_in[j], 16 * (i + 1))
                wait(pe, hidden_ready, k - 1)
                pe.matmul(ps[0:HID, H_BANK + h, :], w1_s[32 * j:32 * j + 32, :],
                          ef[32 * j:32 * j + 32, 512 * h:512 * h + 512], start=True, stop=True,
                          tile_position=(32 * j, 0)).then_inc(hidden_psum, 1)

            def weights(i, j, h):
                if beyond(i, j, h):
                    return
                k = 2 * (RING * i + j) + h
                pe.wait_ge(hidden_ready, k + 1)
                wait(pe, weights_used, k - 1)
                for t in range(4):
                    mm = pe.matmul(w_ps[h][:, t, :], hid[:, h, P * t:P * t + P], w2_s[:, :], start=True, stop=True)
                mm.then_inc(weights_ready, 1)

            def messages_of(b):
                return [lambda t: prod_a[:, b, t, :], lambda t: msg_b[:, b, t, :]]

            def layer2(i):
                for j in range(RING):
                    c = RING * i + j
                    b = j % 2
                    hidden(*half(i, j, 3))
                    weights(*half(i, j, 2))
                    hidden(*half(i, j, 4))
                    weights(*half(i, j, 3))
                    if not (isinstance(c, int) and c == 0):
                        more_windows(c - 1, messages_of(1 - b), j, 1 - b, 1)
                    pe.wait_ge(messages_ready, c + 1)
                    wait(pe, added2, c - 1)
                    segment_sums(lambda t: onehot[:, b, t, :], messages_of(b), j, b, seg2_done, 1)

            hidden(0, 0, 0)
            hidden(0, 0, 1)
            pe.wait_ge(setup_done, 3)
            weights(0, 0, 0)
            hidden(0, 1, 0)
            weights(0, 0, 1)
            pe.wait_ge(turned_used, -(-NR // 4))
            over_iterations(pe, layer2)
            more_windows(CHUNKS - 1, messages_of((CHUNKS - 1) % 2), 0, (CHUNKS - 1) % 2, 1)

            pe.wait_ge(added2, CHUNKS + 1)
            accb_cols = acc_b[:, 0:NODES].rearrange("f (p r) -> f r p", r=NR)
            for n in range(-(-NR // FIN_R)):
                r0, r1 = n * FIN_R, min(NR, n * FIN_R + FIN_R)
                for r in range(r0, r1):
                    dest = ps[:, n, (r - r0) * FEAT:(r - r0 + 1) * FEAT]
                    pe.matmul(dest, acc_cols[:, r, :], sel_a_s[:, :], start=True, stop=False)
                    mm = pe.matmul(dest, accb_cols[0:96, r, :], sel_b_s[:, :], start=False, stop=True)
                mm.then_inc(fin_ready, 1)

        @block.vector
        def _(dve):
            extra = dve.alloc_register("dve_extra")
            copied = dve.alloc_register("dve_copied")
            dve.reg_mov(extra, 0)
            dve.reg_mov(copied, 0)
            chain = [0]

            def link(ins):
                chain[0] += 1
                ins.then_inc(dve_chain, 1)
                dve.wait_ge(dve_chain, chain[0])

            def rows(ap, n):
                return ap[:, :, None].to_broadcast([P, NR, n])

            dve.wait_ge(dstc_loaded, 16)
            dve.tensor_reduce(mm_c[:, 0, :], dst_c[:, :, :], AX, ALU.min).then_inc(bounds_done, 1)
            dve.tensor_reduce(mm_c[:, 1, :], dst_c[:, :, :], AX, ALU.max).then_inc(bounds_done, 1)

            dve.memset(w2_s[:, :], 0.0).then_inc(params_clear, 1)
            dve.memset(zero_b, 0.0).then_inc(setup_done, 1)
            dve.wait_ge(src_loaded, 16)
            link(dve.tensor_copy(src_f, src_i))
            tmp = hn[:, :, :].rearrange("p r f -> p (r f)")[:, 0:T_ALL]
            link(dve.tensor_scalar(tmp, src_f, 1.0 / NR, -(NR - 1) / 2.0 / NR, ALU.mult, ALU.add))
            link(dve.tensor_scalar(tmp, tmp, RNE, -RNE, ALU.add, ALU.add))
            link(dve.tensor_copy(dig_p, tmp))
            link(dve.scalar_tensor_tensor(out=dig_r, in0=tmp, scalar=-float(NR), in1=src_f, op0=ALU.mult, op1=ALU.add))
            dve.wait_ge(iota_done, 3)

            def count(i):
                for b in range(2):
                    n = 2 * i + b
                    wait(dve, hist_used, n - 1)
                    for iota, dig, oh, m in ((iota_p, dig_p, oh_p, P), (iota_r, dig_r, oh_r, NR)):
                        ins = dve.tensor_tensor(oh[:, b, :, :], iota,
                                                dig[:, None, bass.ds(n * HB, HB)].to_broadcast([P, m, HB]),
                                                ALU.is_equal)
                    ins.then_inc(hist_ready, 1)

            count(0)
            with dve.Fori(1, HBATCH // 2) as i:
                count(i)

            dve.wait_ge(dst_loaded, 16)
            dve.wait_ge(bounds_in, 32)
            link(dve.tensor_copy(dst_rel[:, :], dst_i))
            link(dve.tensor_tensor(dst_rel[:, :].rearrange("p (c t) -> p c t", t=TILES),
                                   dst_rel[:, :].rearrange("p (c t) -> p c t", t=TILES),
                                   bound[:, 0, :, None].to_broadcast([P, CHUNKS, TILES]), ALU.subtract))
            link(dve.tensor_copy(row_i[:, 0, :], bound[0:1, 0, :]))
            link(dve.tensor_tensor(row_i[:, 1, :], bound[0:1, 1, :], bound[0:1, 0, :], ALU.subtract))
            link(dve.memset(acc_a[:, :], 0.0))
            link(dve.memset(g[:, :, :, FEAT:FEAT + 1], 1.0))

            roots = [0]

            def rsqrt(v, y):
                roots[0] += 1
                dve.sem_inc(root_asked, 1)
                dve.wait_ge(root_given, roots[0])
                t = stat[:, 0, :]
                link(dve.reciprocal(y, root[:, :]))
                link(dve.tensor_tensor(t, y, y, ALU.mult))
                link(dve.tensor_tensor(t, t, v, ALU.mult))
                link(dve.tensor_scalar(t, t, -0.5, 1.5, ALU.mult, ALU.add))
                link(dve.tensor_tensor(y, y, t, ALU.mult))

            def centre():
                link(dve.tensor_reduce(stat[:, 0, :], x[:, :, :], AX, ALU.add))
                link(dve.tensor_scalar(stat[:, 1, :], stat[:, 0, :], -1.0 / FEAT, None, ALU.mult))
                link(dve.tensor_tensor(xc[:, :, :], x[:, :, :], rows(stat[:, 1, :], FEAT), ALU.add))
                link(dve.tensor_tensor(hn[:, :, :], xc[:, :, :], xc[:, :, :], ALU.mult))
                link(dve.tensor_reduce(stat[:, 0, :], hn[:, :, :], AX, ALU.add))
                link(dve.tensor_scalar(stat[:, 1, :], stat[:, 0, :], 1.0 / FEAT, EPS, ALU.mult, ALU.add))
                rsqrt(stat[:, 1, :], stat[:, 2, :])

            dve.wait_ge(x_loaded, 16)
            centre()
            dve.wait_ge(degrees_done, 1)
            link(dve.tensor_scalar(stat[:, 1, :], ps[:, H_BANK, 0:NR], 1.0, None, ALU.max))
            rsqrt(stat[:, 1, :], norm_src[:, :])
            link(dve.tensor_tensor(stat[:, 3, :], stat[:, 2, :], norm_src[:, :], ALU.mult))
            dve.scalar_tensor_tensor(out=hn[:, :, :], in0=xc[:, :, :], scalar=0.0, in1=rows(stat[:, 3, :], FEAT),
                                     op0=ALU.max, op1=ALU.mult).then_inc(table1_ready, 1)
            link(dve.memset(acc_b[:, :], 0.0))
            link(dve.memset(hid[HID:P, :, :], 0.0))
            dve.memset(hid[HID:HID + 1, :, :], 1.0).then_inc(setup_done, 1)

            def make_onehot(c, b, done):
                dve.tensor_tensor(onehot[:, b, :, :], iota_w[:, None, :].to_broadcast([P, TILES, WIN]),
                                  dst_rel[:, bass.ds(c * TILES, TILES)][:, :, None].to_broadcast([P, TILES, WIN]),
                                  ALU.is_equal).then_inc(done, 1)

            def add_sums(at, b, layer, done):
                if layer == 0:
                    parts = [(acc_a, FEAT + 1, 0)]
                else:
                    parts = [(acc_a, P, 0), (acc_b, MW, 128)]
                for acc, m, col in parts:
                    here = acc[0:m, bass.ds(at, WIN)]
                    ins = dve.tensor_tensor(here, here, ps[0:m, S_BANK + b, col:col + WIN], ALU.add)
                ins.then_inc(done, 1)

            def bounds_of(c):
                return (dve.value_load(row_i[0:1, 0, bass.ds(c, 1)], min_val=0, max_val=NODES - 1),
                        dve.value_load(row_i[0:1, 1, bass.ds(c, 1)], min_val=0, max_val=NODES))

            def more_windows(c, b, base, span, layer):
                with dve.If(span > WIN - 1):
                    dve.reg_add(copied, copied, 1)
                    dve.tensor_copy(dst_x[:, :], dst_rel[:, bass.ds(c * TILES, TILES)]).then_inc(x_copied, 1)
                    with dve.Fori(WIN, span + 1, WIN) as off:
                        dve.wait_ge(x_copied, dve.snap(copied))
                        dve.reg_add(extra, extra, 1)
                        n = dve.snap(extra)
                        dve.tensor_scalar(dst_x[:, :], dst_x[:, :], -float(WIN), None, ALU.add).then_inc(x_shifted, 1)
                        dve.wait_ge(x_shifted, n)
                        dve.tensor_tensor(onehot_x[:, :, :], iota_w[:, None, :].to_broadcast([P, TILES, WIN]),
                                          dst_x[:, :, None].to_broadcast([P, TILES, WIN]),
                                          ALU.is_equal).then_inc(x_onehot, 1)
                        dve.wait_ge(x_seg, n)
                        at = nc.s_assert_within(base + off, min_val=0, max_val=NODES - 1)
                        add_sums(at, b, layer, x_added)
                        dve.wait_ge(x_added, n)

            make_onehot(0, 0, onehot1_ready)

            def layer1(i):
                for j in range(RING):
                    c = RING * i + j
                    b = j % 2
                    if not (isinstance(c, int) and c == CHUNKS - 1):
                        make_onehot(c + 1, 1 - b, onehot1_ready)
                    base, span = bounds_of(c)
                    dve.wait_ge(seg1_done, c + 1)
                    wait(dve, added1, c)
                    add_sums(base, b, 0, added1)
                    more_windows(c, b, base, span, 0)

            over_iterations(dve, layer1)
            dve.wait_ge(added1, CHUNKS)
            dve.memset(stat[:, 0, 0:1], 0.0).then_inc(added1, 1)

            dve.wait_ge(par_loaded, 16 * N_PARAMS)
            def mid_bank(n):
                r0, r1 = n * MID_R, min(NR, n * MID_R + MID_R)
                return r0, r1, ps[:, n, 0:(r1 - r0) * (FEAT + 1)].rearrange("p (r f) -> p r f", f=FEAT + 1)

            for n in range(-(-NR // MID_R)):
                r0, r1, z = mid_bank(n)
                dve.wait_ge(mid_ready, n + 1)
                link(dve.tensor_scalar(stat[:, 1, r0:r1], z[:, :, FEAT], 1.0, None, ALU.max))
            rsqrt(stat[:, 1, :], stat[:, 3, :])
            for n in range(-(-NR // MID_R)):
                r0, r1, z = mid_bank(n)
                link(dve.tensor_tensor(xc[:, r0:r1, :], z[:, :, 0:FEAT],
                                       stat[:, 3, r0:r1, None].to_broadcast([P, r1 - r0, FEAT]), ALU.mult))
            link(dve.tensor_tensor(xc[:, :, :], xc[:, :, :], b_l0_s[:, None, :].to_broadcast([P, NR, FEAT]), ALU.add))
            link(dve.scalar_tensor_tensor(out=x[:, :, :], in0=xc[:, :, :], scalar=0.0, in1=x[:, :, :],
                                          op0=ALU.max, op1=ALU.add))
            dve.wait_ge(table1_out, 16)
            centre()
            link(dve.scalar_tensor_tensor(out=hn[:, :, 0:MUL], in0=xc[:, :, 0:MUL], scalar=0.0,
                                          in1=rows(stat[:, 2, :], MUL), op0=ALU.max, op1=ALU.mult))
            for m in range(3):
                ins = dve.scalar_tensor_tensor(
                    out=hn[:, :, MUL + MUL * m:MUL + MUL * m + MUL], in0=xc[:, :, MUL + m:FEAT:3], scalar=0.0,
                    in1=rows(stat[:, 2, :], MUL), op0=ALU.max, op1=ALU.mult)
            ins.then_inc(table2_ready, 1)
            link(dve.memset(acc_a[:, :], 0.0))
            link(dve.tensor_scalar(w2_s[:, 0:64], w2_s[:, 0:64], float(ALPHA * C110), None, ALU.mult))
            link(dve.tensor_scalar(w2_s[:, 64:256], w2_s[:, 64:256], float(ALPHA), None, ALU.mult))
            dve.tensor_scalar(sel_b_s[64:96, :], sel_b_s[64:96, :], float(SI_SCALE), None,
                              ALU.mult).then_inc(setup_done, 1)

            def d_coefs(i, j):
                c = RING * i + j
                b = j % 2
                make_onehot(c, b, x_dummy)
                dve.wait_ge(coefs_ready, c + 1)
                dve.tensor_tensor(vsh[:, :, :, :], g[:, j, :, MUL:FEAT].rearrange("p t (m i) -> p t i m", m=3),
                                  sh[:, j, :, None, 1:4].to_broadcast([P, TILES, MUL, 3]),
                                  ALU.mult).then_inc(vsh_ready, 1)
                dve.wait_ge(vsh_ready, c + 1)
                dve.tensor_reduce(q[:, b, :, 0:MUL], vsh[:, :, :, :], AX, ALU.add).then_inc(d_ready, 1)

            x_dummy = sem("onehot2_ready")

            def products(c, j, h):
                k = 2 * c + h
                b = j % 2
                w = w_ps[h]
                qt = q[:, b, 4 * h:4 * h + 4, :]
                dve.wait_ge(weights_ready, k + 1)
                dve.tensor_tensor(
                    prod_b[:, h, :, 0:3, :].rearrange("p t m (i o) -> p t m i o", o=MUL),
                    w[:, :, 128:192].rearrange("p t (i o) -> p t i o", o=MUL)[:, :, None, :, :].to_broadcast([P, 4, 3, MUL, MUL]),
                    qt[:, :, 16:40].rearrange("p t (m i) -> p t m i", m=3)[:, :, :, :, None].to_broadcast([P, 4, 3, MUL, MUL]),
                    ALU.mult)
                dve.tensor_tensor(
                    prod_b[:, h, :, 3, :].rearrange("p t (i o) -> p t i o", o=MUL),
                    w[:, :, 192:256].rearrange("p t (i o) -> p t i o", o=MUL),
                    qt[:, :, 40:48, None].to_broadcast([P, 4, MUL, MUL]), ALU.mult).then_inc(prodb_ready, 1)
                if h == 0:
                    dve.wait_ge(d_ready, c + 1)
                dve.tensor_tensor(
                    prod_a[:, b, 4 * h:4 * h + 4, :].rearrange("p t (k o) -> p t k o", o=MUL),
                    w[:, :, 0:128].rearrange("p t (k o) -> p t k o", o=MUL),
                    qt[:, :, 0:16, None].to_broadcast([P, 4, 16, MUL]), ALU.mult).then_inc(weights_used, 1)
                dve.wait_ge(prodb_ready, k + 1)
                dve.tensor_reduce(
                    msg_b[:, b, 4 * h:4 * h + 4, 0:32].rearrange("p t (g o) -> p t g o", o=MUL),
                    prod_b[:, h, :, :, :].rearrange("p t g (i o) -> p t g o i", o=MUL),
                    AX, ALU.add).then_inc(reduced, 1)

            def finish_messages(c, j):
                b = j % 2
                dve.wait_ge(reduced, 2 * c + 2)
                dve.tensor_tensor(
                    msg_b[:, b, :, 32:56].rearrange("p t (m o) -> p t m o", m=3),
                    msg_b[:, b, :, None, 24:32].to_broadcast([P, TILES, 3, MUL]),
                    sh[:, j, :, 1:4, None].to_broadcast([P, TILES, 3, MUL]), ALU.mult).then_inc(messages_ready, 1)

            def join_sums(c, b, base, span):
                dve.wait_ge(seg2_done, c + 1)
                wait(dve, added2, c)
                add_sums(base, b, 1, added2)
                more_windows(c, b, base, span, 1)

            def layer2(i):
                for j in range(RING):
                    c = RING * i + j
                    b = j % 2
                    first = isinstance(c, int) and c == 0
                    if not first:
                        limits = bounds_of(c - 1)
                    products(c, j, 1)
                    if not first:
                        join_sums(c - 1, 1 - b, *limits)
                    finish_messages(c, j)
                    if not (isinstance(c, int) and c == CHUNKS - 1):
                        nxt = (i, j + 1) if j + 1 < RING else (i + 1, 0)
                        d_coefs(*nxt)
                        products(c + 1, nxt[1], 0)

            d_coefs(0, 0)
            products(0, 0, 0)
            over_iterations(dve, layer2)
            join_sums(CHUNKS - 1, (CHUNKS - 1) % 2, *bounds_of(CHUNKS - 1))
            dve.wait_ge(added2, CHUNKS)
            dve.memset(stat[:, 0, 0:1], 0.0).then_inc(added2, 1)

            for n in range(-(-NR // FIN_R)):
                r0, r1 = n * FIN_R, min(NR, n * FIN_R + FIN_R)
                dve.wait_ge(fin_ready, n + 1)
                dve.tensor_tensor(xc[:, r0:r1, :], x[:, r0:r1, :],
                                  ps[:, n, 0:(r1 - r0) * FEAT].rearrange("p (r f) -> p r f", f=FEAT),
                                  ALU.add).then_inc(out_ready, 1)


def selections():
    a = np.zeros((P, FEAT), np.float32)
    b = np.zeros((64, FEAT), np.float32)
    for o in range(MUL):
        a[o::MUL, o] = 1.0
        for m in range(3):
            b[m * MUL + o, MUL + 3 * o + m] = 1.0
            b[32 + m * MUL + o, MUL + 3 * o + m] = 1.0
    return a, b


def kernel(x, src, dst, edge_attr_32, edge_attr_4, L0_gnn_weight, L0_gnn_bias, L1_gnn_W1, L1_gnn_b1,
           L1_gnn_W2, L1_gnn_b2, L1_gnn_si_w0, L1_gnn_si_w1):
    import concourse.bacc as bacc
    from concourse.bass_utils import run_bass_kernel_spmd

    edges = CHUNKS * CHUNK
    pad = edges - N_EDGES
    xn = np.pad(np.asarray(x), ((0, NODES - N_NODES), (0, 0))).reshape(P, NR * FEAT)
    s = np.pad(np.asarray(src), (0, pad), constant_values=NODES - 1)
    d = np.pad(np.asarray(dst), (0, pad), constant_values=N_NODES)
    ea = np.pad(np.asarray(edge_attr_32), ((0, pad), (0, 0))).reshape(CHUNKS, CHUNK, FEAT).transpose(0, 2, 1)
    e4 = np.pad(np.asarray(edge_attr_4), ((0, pad), (0, 0))).reshape(CHUNKS, TILES, P, 4).transpose(0, 2, 1, 3)
    w0 = np.zeros((FEAT + 1, FEAT + 1), np.float32)
    w0[:FEAT, :FEAT] = L0_gnn_weight
    w0[FEAT, FEAT] = 1.0
    mm = MUL * MUL
    w2 = np.concatenate([np.asarray(L1_gnn_W2), np.asarray(L1_gnn_b2)[None, :]])
    w2 = np.concatenate([w2[:, 3 * mm:], w2[:, :mm], w2[:, 2 * mm:3 * mm], w2[:, mm:2 * mm]], axis=1)
    skip = np.zeros((FEAT, FEAT), np.float32)
    skip[:MUL, :MUL] = L1_gnn_si_w0
    for m in range(3):
        skip[MUL + MUL * m:MUL + MUL * m + MUL, MUL + m::3] = L1_gnn_si_w1
    sel_a, sel_b = selections()
    arrays = {
        "x_nodes": xn,
        "src_all": s.reshape(CHUNKS * TILES, P).T,
        "src_chunks": s.reshape(CHUNKS, TILES, P).transpose(0, 2, 1),
        "dst_all": d.reshape(CHUNKS * TILES, P).T,
        "dst_chunks": d.reshape(CHUNKS, CHUNK),
        "edge_t": ea,
        "sh_chunks": e4.reshape(CHUNKS, P, TILES * 4),
        "w_l0": w0,
        "b_l0": np.asarray(L0_gnn_bias)[None, :],
        "w1": np.asarray(L1_gnn_W1),
        "b1": np.asarray(L1_gnn_b1)[:, None],
        "w2": w2,
        "skip_w": skip,
        "sel_a": sel_a,
        "sel_b": sel_b,
        "ident_in": np.eye(P, dtype=np.float32),
    }
    arrays = {k: np.ascontiguousarray(v) for k, v in arrays.items()}
    nc = bacc.Bacc("TRN2", target_bir_lowering=False, num_devices=1)
    aps = {k: nc.dram_tensor(k, v.shape, mybir.dt.from_np(v.dtype), kind="ExternalInput").ap()
           for k, v in arrays.items()}
    out = nc.dram_tensor("out", (NODES, FEAT), F32, kind="ExternalOutput").ap()
    gnn_program(nc, **aps, out=out)
    r = run_bass_kernel_spmd(nc, [arrays], core_ids=[0])
    return r.results[0]["out"][:N_NODES]
```

```python
from contextlib import ExitStack

import numpy as np
import concourse.bass as bass
from concourse import mybir

ALU = mybir.AluOpType
ACT = mybir.ActivationFunctionType
F32 = mybir.dt.float32
BF16 = mybir.dt.bfloat16
I32 = mybir.dt.int32
AX = mybir.AxisListType.X

P = 128
N_NODES, N_EDGES = 12500, 212500
FEAT, HID, MUL = 32, 64, 8
NR = -(-N_NODES // P)
NODES = P * NR
TILES = 8
CHUNK = TILES * P
RING = 4
CHUNKS = -(-N_EDGES // (CHUNK * RING)) * RING
ITERS = CHUNKS // RING
WIN = 68
ACC_W = NODES + WIN
EARLY = 28
EARLY_ITERS = EARLY // RING
A_ITERS = EARLY // 2
A_UNITS = A_ITERS * (RING + 2)
REG_ITERS = ITERS - EARLY_ITERS
UNITS = ((0, 0), (0, 1), (1, 0), (0, 2), (0, 3), (1, 1))
N_PARAMS = 8 + RING
EPS = 1e-5
ALPHA, C110, SI_SCALE = 0.25, 1.0 / np.sqrt(3.0), 1.0 / np.sqrt(float(MUL))
HB = 16
HBATCH = CHUNKS * TILES // HB
RNE = 12582912.0
MID_R = 15
FIN_R = 16
MW = 56


def gnn_program(nc, x_nodes, src_all, src_chunks, src_rows, dst_all, dst_chunks, edge_t, sh_chunks,
                w_l0, b_l0, w1, b1, w2, skip_w, sel_a, sel_b, ident_in, out):
    assert EARLY % RING == 0 and REG_ITERS > A_ITERS + 1
    assert CHUNKS % (2 * HB // TILES) == 0 and CHUNKS % 2 == 0
    with ExitStack() as ctx:
        def sb(name, shape, dt=F32):
            return ctx.enter_context(nc.sbuf_tensor(name, shape, dt))

        def sem(name):
            return ctx.enter_context(nc.semaphore(name))

        table1 = nc.dram_tensor("table1", [NODES, FEAT], F32).ap()
        table0 = nc.dram_tensor("table0", [NODES, FEAT], F32).ap()
        table2 = nc.dram_tensor("table2", [NODES, FEAT], F32).ap()
        bounds = nc.dram_tensor("bounds", [2, CHUNKS], F32).ap()

        ps = ctx.enter_context(nc.psum_tensor("ps", [P, 8, 512], F32))
        W_BANK, H_BANK, S_BANK = 0, 4, 6

        acc_a = sb("acc_a", [P, ACC_W])
        acc_b = sb("acc_b", [P, ACC_W])
        x = sb("x", [P, NR, FEAT])
        xc = sb("xc", [P, NR, FEAT])
        hn = sb("hn", [P, NR, FEAT])
        stat = sb("stat", [P, 4, NR])
        norm_src = sb("norm_src", [P, NR])
        root = sb("root", [P, NR])
        dst_rel = sb("dst_rel", [P, CHUNKS * TILES])
        bound = sb("bound", [P, 2, CHUNKS])
        row_i = sb("row_i", [1, 2, CHUNKS], I32)
        dst_c = sb("dst_c", [CHUNKS // 2, 2, CHUNK], I32)
        mm_c = sb("mm_c", [CHUNKS // 2, 2, 2])
        iota_all = sb("iota_all", [P, NR])
        part_rne = sb("part_rne", [P, 1])
        idx = sb("idx", [P, RING, TILES], I32)
        g = sb("g", [P, RING, TILES, FEAT + 1])
        sh = sb("sh", [P, RING, TILES, 4])
        onehot = sb("onehot", [P, 2, TILES, WIN])
        onehot_x = sb("onehot_x", [P, TILES, WIN])
        dst_x = sb("dst_x", [P, TILES])
        ef = sb("ef", [P, CHUNK])
        hid = sb("hid", [P, 2, 512])
        q = sb("q", [P, 2, TILES, 48])
        vsh = sb("vsh", [P, TILES, MUL, 3])
        prod_a = sb("prod_a", [P, 2, TILES, 128])
        prod_b = sb("prod_b", [P, 2, 4, 4, 64])
        msg_b = sb("msg_b", [P, 2, TILES, MW])
        ident = sb("ident", [P, P])
        w_l0_s = sb("w_l0_s", [FEAT + 1, FEAT + 1])
        b_l0_s = sb("b_l0_s", [P, FEAT])
        w1_s = sb("w1_s", [P, HID])
        b1_s = sb("b1_s", [HID, 1])
        w2_s = sb("w2_s", [P, 4 * MUL * MUL])
        sel_a_s = sb("sel_a_s", [P, FEAT])
        sel_b_s = sb("sel_b_s", [96, FEAT])

        hist = acc_b[:, :].bitcast(BF16)
        T_ALL = CHUNKS * TILES
        o = 0
        dig_p, o = hist[:, o:o + T_ALL], o + T_ALL
        dig_r, o = hist[:, o:o + T_ALL], o + T_ALL
        oh_p, o = hist[:, o:o + 2 * P * HB].rearrange("p (b j t) -> p b j t", b=2, t=HB), o + 2 * P * HB
        oh_r, o = hist[:, o:o + 2 * NR * HB].rearrange("p (b j t) -> p b j t", b=2, t=HB), o + 2 * NR * HB
        zero_b, o = hist[:, o:o + P], o + P
        early_at = -(-o // 2)
        early = acc_b[:, early_at:early_at + EARLY * TILES * FEAT]
        assert early_at + EARLY * TILES * FEAT <= ACC_W
        iotas = prod_a[:, :, :, :].rearrange("p b t k -> p (b t k)").bitcast(BF16)
        iota_p = iotas[:, 0:P * HB].rearrange("p (j t) -> p j t", t=HB)
        iota_r = iotas[:, P * HB:(P + NR) * HB].rearrange("p (j t) -> p j t", t=HB)
        dst_i, src_i, src_f, tmp = (acc_a[:, k * T_ALL:(k + 1) * T_ALL] for k in range(4))
        dst_i, src_i = dst_i.bitcast(I32), src_i.bitcast(I32)
        flat_b = prod_b[:, :, :, :, :].rearrange("p h t g k -> p (h t g k)")
        early_src = ef[:, :].bitcast(I32)
        early_div = flat_b[:, 0:CHUNK]
        early_sel = flat_b[:, CHUNK:CHUNK + TILES * NR].rearrange("p (t r) -> p t r", r=NR)
        early_p = hid[:, :, :].rearrange("p b e -> p (b e)")
        early_r = msg_b[:, :, :, :].rearrange("p b t k -> p (b t k)")[:, 0:TILES * NR].rearrange(
            "p (t r) -> p t r", r=NR)
        flat_q = q[:, :, :, :].rearrange("p b t k -> p (b t k)")
        early_g = flat_q[:, 0:TILES * (FEAT + 1)].rearrange("p (t f) -> p t f", f=FEAT + 1)
        early_norm = flat_q[:, TILES * (FEAT + 1):TILES * (FEAT + 2)]

        src_loaded, dst_loaded, dstc_loaded, x_loaded, par_loaded = (
            sem(n) for n in ("src_loaded", "dst_loaded", "dstc_loaded", "x_loaded", "par_loaded"))
        bounds_done, bounds_out, bounds_in = sem("bounds_done"), sem("bounds_out"), sem("bounds_in")
        iota_done = sem("iota_done")
        hist_ready, hist_used, degrees_done = sem("hist_ready"), sem("hist_used"), sem("degrees_done")
        dve_chain = sem("dve_chain")
        params_clear = sem("params_clear")
        zero_ready, acc_a_clear, weights_scaled = sem("zero_ready"), sem("acc_a_clear"), sem("weights_scaled")
        table0_ready, table0_out = sem("table0_ready"), sem("table0_out")
        kept = sem("kept")
        early_src_in, early_divided = sem("early_src_in"), sem("early_divided")
        early_p_ready, early_norm_psum, early_g_ready = (
            sem("early_p_ready"), sem("early_norm_psum"), sem("early_g_ready"))
        table1_ready, table1_out = sem("table1_ready"), sem("table1_out")
        table2_ready, table2_out = sem("table2_ready"), sem("table2_out")
        idx_in = [sem(f"idx_in{j}") for j in range(RING)]
        sh_in = [sem(f"sh_in{j}") for j in range(RING)]
        ef_in = [sem(f"ef_in{j}") for j in range(RING)]
        gathered = [sem(f"gathered{j}") for j in range(RING)]
        onehot1_ready, seg1_done, added1 = sem("onehot1_ready"), sem("seg1_done"), sem("added1")
        mid_ready = sem("mid_ready")
        hidden_psum, hidden_ready = sem("hidden_psum"), sem("hidden_ready")
        weights_ready, weights_used = sem("weights_ready"), sem("weights_used")
        coefs_ready, vsh_ready, d_ready = sem("coefs_ready"), sem("vsh_ready"), sem("d_ready")
        prodb_ready, reduced, messages_ready = sem("prodb_ready"), sem("reduced"), sem("messages_ready")
        seg2_done, added2 = sem("seg2_done"), sem("added2")
        turned, turned_used = sem("turned"), sem("turned_used")
        acc_b_clear = sem("acc_b_clear")
        slots_opened = sem("slots_opened")
        root_asked, root_given = sem("root_asked"), sem("root_given")
        x_copied, x_shifted, x_onehot, x_seg, x_added = (
            sem(n) for n in ("x_copied", "x_shifted", "x_onehot", "x_seg", "x_added"))
        fin_ready, out_ready, out_stored = sem("fin_ready"), sem("out_ready"), sem("out_stored")

        def wait(eng, s, value):
            if not isinstance(value, int) or value > 0:
                eng.wait_ge(s, value)

        def over_iterations(eng, body):
            body(0)
            with eng.Fori(1, ITERS - 1) as i:
                body(i)
            body(ITERS - 1)

        GATH = 16 * TILES
        w_ps = [ps[:, W_BANK + 2 * b:W_BANK + 2 * b + 2, :].rearrange("p b (u w) -> p (b u) w", w=256)
                for b in range(2)]
        block = ctx.enter_context(nc.Block())

        @block.sync
        def _(sp):
            sp.dma_start(x[:, :, :], x_nodes.rearrange("p (r f) -> p r f", f=FEAT)).then_inc(x_loaded, 16)
            sp.dma_start(src_i, src_all).then_inc(src_loaded, 16)
            sp.dma_start(dst_c[:, :, :], dst_chunks.rearrange("(q s) e -> q s e", s=2)).then_inc(dstc_loaded, 16)
            sp.dma_start(dst_i, dst_all).then_inc(dst_loaded, 16)
            sp.dma_start(w_l0_s[:, :], w_l0).then_inc(par_loaded, 16)
            sp.dma_start(b_l0_s[:, :], b_l0.to_broadcast([P, FEAT])).then_inc(par_loaded, 16)
            for j in range(RING):
                sp.dma_start(w1_s[32 * j:32 * j + 32, :], w1).then_inc(par_loaded, 16)
            sp.dma_start(b1_s[:, :], b1).then_inc(par_loaded, 16)
            sp.wait_ge(params_clear, 1)
            sp.dma_start(w2_s[0:HID + 1, :], w2).then_inc(par_loaded, 16)
            sp.dma_start(sel_a_s[:, :], sel_a).then_inc(par_loaded, 16)
            sp.dma_start(sel_b_s[0:64, :], sel_b).then_inc(par_loaded, 16)
            sp.dma_start(sel_b_s[64:96, :], skip_w).then_inc(par_loaded, 16)
            sp.dma_start(ident[:, :], ident_in).then_inc(par_loaded, 16)
            for j in range(RING):
                sp.dma_start(idx[:, j, :], src_chunks[j]).then_inc(idx_in[j], 16)

            def load1(i):
                for j in range(RING):
                    sp.wait_ge(gathered[j], GATH * (i + 1))
                    sp.dma_start(idx[:, j, :], load_from(src_chunks, RING * i + RING + j)).then_inc(idx_in[j], 16)

            def load_from(dram, c):
                return dram[c] if isinstance(c, int) else dram[bass.ds(c, 1)].rearrange("a p k -> (a p) k")

            with sp.Fori(0, EARLY_ITERS - 1) as i:
                load1(i)
            sp.dma_start(early_src, src_rows[0:1, :].to_broadcast([P, CHUNK])).then_inc(early_src_in, 16)
            sp.wait_ge(bounds_done, 2)
            for k in range(2):
                sp.dma_start(bounds[k:k + 1, :].rearrange("a (q s) -> (a q) s", s=2), mm_c[:, k, :]).then_inc(bounds_out, 16)
            sp.wait_ge(bounds_out, 32)
            for k in range(2):
                sp.dma_start(bound[:, k, :], bounds[k:k + 1, :].to_broadcast([P, CHUNKS])).then_inc(bounds_in, 16)
            with sp.Fori(EARLY_ITERS - 1, ITERS - 1) as i:
                load1(i)
            sp.wait_ge(early_divided, EARLY)
            for j in range(RING):
                sp.dma_start(sh[:, j, :, :], sh_chunks[j].rearrange("p (t d) -> p t d", d=4)).then_inc(sh_in[j], 16)
                sp.dma_start(ef[32 * j:32 * j + 32, :], edge_t[j]).then_inc(ef_in[j], 16)
            for j in range(RING):
                sp.wait_ge(gathered[j], GATH * ITERS)
                sp.dma_start(idx[:, j, :], src_chunks[j]).then_inc(idx_in[j], 16)
            with sp.Fori(0, ITERS - 1) as i:
                for j in range(RING):
                    c = RING * i + j
                    sp.wait_ge(hidden_psum, 2 * c + 2)
                    sp.dma_start(ef[32 * j:32 * j + 32, :], load_from(edge_t, c + RING)).then_inc(ef_in[j], 16)
                    sp.wait_ge(gathered[j], GATH * (i + ITERS + 1))
                    sp.dma_start(idx[:, j, :], load_from(src_chunks, c + RING)).then_inc(idx_in[j], 16)
                    sp.wait_ge(messages_ready, c + 1)
                    sp.dma_start(sh[:, j, :, :].rearrange("p t d -> p (t d)"),
                                 load_from(sh_chunks, c + RING)).then_inc(sh_in[j], 16)
            for n in range(-(-NR // FIN_R)):
                sp.wait_ge(out_ready, n + 1)
                r0, r1 = n * FIN_R, min(NR, n * FIN_R + FIN_R)
                sp.dma_start(out.rearrange("(p r) f -> p r f", p=P)[:, r0:r1, :], xc[:, r0:r1, :]).then_inc(out_stored, 16)
            sp.wait_ge(out_stored, 16 * -(-NR // FIN_R))

        @block.gpsimd
        def _(pool):
            pool.iota(iota_p, [[1, P], [0, HB]], base=0, channel_multiplier=0,
                      allow_small_or_imprecise_dtypes=True).then_inc(iota_done, 1)
            pool.iota(iota_r, [[1, NR], [0, HB]], base=0, channel_multiplier=0,
                      allow_small_or_imprecise_dtypes=True).then_inc(iota_done, 1)
            pool.iota(iota_all[:, :], [[1, NR]], base=0, channel_multiplier=0,
                      allow_small_or_imprecise_dtypes=True).then_inc(iota_done, 1)
            pool.iota(part_rne[:, :], [[1, 1]], base=0, channel_multiplier=1,
                      allow_small_or_imprecise_dtypes=True).then_inc(iota_done, 1)

            def gather(i, table, iteration, free):
                for j in range(RING):
                    pool.wait_ge(idx_in[j], 16 * (iteration + 1))
                    free(RING * i + j, j)
                    pool.sem_inc(slots_opened, 1)
                    for t in range(TILES):
                        pool.indirect_dma_start(
                            out=g[:, j, t, 0:FEAT], out_offset=None, in_=table,
                            in_offset=bass.IndirectOffsetOnAxis(ap=idx[:, j, t:t + 1], axis=0),
                        ).then_inc(gathered[j], 16)

            def kept_four_before(c, j):
                wait(pool, kept, c - RING + 1)

            def used_in(first_unit, per_iteration, position):
                def free(i):
                    return lambda c, j: pool.wait_ge(
                        onehot1_ready, first_unit + per_iteration * i + position[j] + 3)
                return free

            pool.wait_ge(table0_out, 16)
            gather(0, table0, 0, kept_four_before)
            with pool.Fori(1, EARLY_ITERS) as i:
                gather(i, table0, i, kept_four_before)
            pool.wait_ge(table1_out, 16)
            gather(EARLY_ITERS, table1, EARLY_ITERS, kept_four_before)
            beside = used_in(0, len(UNITS), [UNITS.index((0, j)) for j in range(RING)])
            alone = used_in(A_UNITS, RING, range(RING))
            with pool.Fori(0, A_ITERS) as i:
                gather(i, table1, i + (EARLY_ITERS + 1), beside(i))
            with pool.Fori(0, REG_ITERS - A_ITERS - 1) as i:
                gather(i, table1, i + (EARLY_ITERS + 1 + A_ITERS), alone(i))

            pool.wait_ge(added1, A_UNITS)
            pool.memset(acc_b[:, :], 0.0).then_inc(acc_b_clear, 1)
            pool.wait_ge(acc_b_clear, 1)
            pool.memset(hid[HID:P, :, :], 0.0).then_inc(acc_b_clear, 1)
            pool.wait_ge(acc_b_clear, 2)
            pool.memset(hid[HID:HID + 1, :, :], 1.0).then_inc(acc_b_clear, 1)

            pool.wait_ge(table2_out, 16)
            over_iterations(pool, lambda i: gather(
                i, table2, i + ITERS, lambda c, j: wait(pool, d_ready, c - RING + 1)))

        @block.scalar
        def _(act):
            def square_root(n):
                act.wait_ge(root_asked, n)
                act.activation(root[:, :], stat[:, 1, :], ACT.Sqrt).then_inc(root_given, 1)

            def keep(i):
                for j in range(RING):
                    act.wait_ge(gathered[j], GATH * (i + 1))
                    dest = early[:, bass.ds((RING * i + j) * (TILES * FEAT), TILES * FEAT)]
                    act.activation(dest.rearrange("p (t f) -> p t f", f=FEAT), g[:, j, :, 0:FEAT],
                                   ACT.Copy).then_inc(kept, 1)

            square_root(1)
            act.wait_ge(table0_ready, 1)
            act.dma_start(table0.rearrange("(p r) f -> p r f", p=P), hn[:, :, :]).then_inc(table0_out, 16)
            with act.Fori(0, EARLY_ITERS - 1) as i:
                keep(i)
            square_root(2)
            act.wait_ge(table1_ready, 1)
            act.dma_start(table1.rearrange("(p r) f -> p r f", p=P), xc[:, :, :]).then_inc(table1_out, 16)
            keep(EARLY_ITERS - 1)

            def divide(e):
                act.wait_ge(early_src_in, 16 * (e + 1))
                wait(act, early_p_ready, e)
                act.activation(early_div, early_src, ACT.Copy, bias=-(NR - 1) / 2.0 / NR,
                               scale=1.0 / NR).then_inc(early_divided, 1)

            def next_sources(e):
                act.wait_ge(early_divided, e + 1)
                row = src_rows[e + 1:e + 2, :] if isinstance(e, int) else src_rows[bass.ds(e + 1, 1), :]
                act.dma_start(early_src, row.to_broadcast([P, CHUNK])).then_inc(early_src_in, 16)

            divide(0)
            next_sources(0)
            with act.Fori(1, EARLY - 1) as e:
                divide(e)
                next_sources(e)
            divide(EARLY - 1)
            square_root(3)
            square_root(4)
            act.wait_ge(table2_ready, 1)
            act.dma_start(table2.rearrange("(p r) f -> p r f", p=P), hn[:, :, :]).then_inc(table2_out, 16)
            act.wait_ge(acc_b_clear, 1)
            for n in range(-(-NR // 4)):
                k = min(4, NR - 4 * n)
                act.wait_ge(turned, n + 1)
                dest = acc_b[64:96, 0:NODES].rearrange("f (p r) -> f r p", r=NR)[:, 4 * n:4 * n + k, :]
                act.activation(dest, ps[0:32, S_BANK + n % 2, 0:128 * k].rearrange("f (r p) -> f r p", p=P),
                               ACT.Copy).then_inc(turned_used, 1)

            def relu(i, j, h):
                if isinstance(i, int) and i >= ITERS:
                    return
                act.wait_ge(hidden_psum, 2 * (RING * i + j) + h + 1)
                act.activation(hid[0:HID, h, :], ps[0:HID, H_BANK + h, :], ACT.Relu,
                               bias=b1_s[:, 0:1]).then_inc(hidden_ready, 1)

            def coefs(i, j):
                if isinstance(i, int) and i >= ITERS:
                    return
                c = RING * i + j
                act.wait_ge(gathered[j], GATH * (i + ITERS + 1))
                act.wait_ge(sh_in[j], 16 * (i + 1))
                wait(act, weights_used, 2 * c - 2)
                for t in range(TILES):
                    act.activation(q[:, j % 2, t, 8:40], g[:, j, t, 0:FEAT], ACT.Copy, scale=sh[:, j, t, 0:1])
                act.activation(q[:, j % 2, :, 40:48], g[:, j, :, 0:MUL], ACT.Copy).then_inc(coefs_ready, 1)

            def after(i, j, n):
                return i + (j + n) // RING, (j + n) % RING

            act.wait_ge(acc_b_clear, 3)
            relu(0, 0, 0)
            relu(0, 0, 1)
            coefs(0, 0)
            relu(0, 1, 0)

            def steps(i):
                for j in range(RING):
                    relu(*after(i, j, 1), 1)
                    coefs(*after(i, j, 1))
                    relu(*after(i, j, 2), 0)

            over_iterations(act, steps)

        @block.tensor
        def _(pe):
            extra = pe.alloc_register("pe_extra")
            pe.reg_mov(extra, 0)

            deg = ps[:, H_BANK, 0:NR]
            pe.wait_ge(zero_ready, 1)
            pe.matmul(deg, zero_b, zero_b[:, 0:NR], start=True, stop=False, skip_group_check=True)

            def count(i):
                for b in range(2):
                    pe.wait_ge(hist_ready, 2 * i + b + 1)
                    for t in range(HB):
                        mm = pe.matmul(deg, oh_p[:, b, :, t], oh_r[:, b, :, t], start=False, stop=False,
                                       skip_group_check=True)
                    mm.then_inc(hist_used, 1)

            with pe.Fori(0, HBATCH // 2) as i:
                count(i)
            pe.matmul(deg, zero_b, zero_b[:, 0:NR], start=False, stop=True,
                      skip_group_check=True).then_inc(degrees_done, 1)

            def segment_sums(oh, lhs, j, b, done, layer):
                groups = [(lhs[0], 0, 0)] if layer == 0 else [(lhs[0], 0, 0), (lhs[1], 128, 1)]
                for rows, col, _ in groups:
                    for t in range(TILES):
                        r = rows(t)
                        m = r.shape[1]
                        mm = pe.matmul(ps[0:m, S_BANK + b, col:col + WIN], r, oh(t),
                                       start=(t == 0), stop=(t == TILES - 1))
                mm.then_inc(done, 1)

            def more_windows(c, lhs, j, b, layer):
                span = pe.value_load(row_i[0:1, 1, bass.ds(c, 1)], min_val=0, max_val=NODES)
                with pe.If(span > WIN - 1):
                    with pe.Fori(WIN, span + 1, WIN):
                        pe.reg_add(extra, extra, 1)
                        pe.wait_ge(x_onehot, pe.snap(extra))
                        segment_sums(lambda t: onehot_x[:, t, :], lhs, j, b, x_seg, layer)

            def take(n, c, j, b, rows):
                lhs = [rows]
                pe.wait_ge(onehot1_ready, n + 1)
                wait(pe, added1, n - 1)
                segment_sums(lambda t: onehot[:, b, t, :], lhs, j, b, seg1_done, 0)
                more_windows(c, lhs, j, b, 0)

            def early_norms(e):
                pe.wait_ge(early_p_ready, e + 1)
                for t in range(TILES):
                    mm = pe.matmul(ps[:, W_BANK + t // 4, NR * (t % 4):NR * (t % 4 + 1)],
                                   early_p[:, P * t:P * (t + 1)], norm_src[:, :], start=True, stop=True)
                mm.then_inc(early_norm_psum, 1)

            def beside_early(i):
                for pos, (is_early, k) in enumerate(UNITS):
                    n = len(UNITS) * i + pos
                    if is_early:
                        pe.wait_ge(early_g_ready, 2 * i + k + 1)
                        take(n, 2 * i + k, 0, pos % 2, lambda t: early_g[:, t, :])
                    else:
                        if UNITS[(pos + 1) % len(UNITS)][0]:
                            early_norms(2 * i + UNITS[pos + 1][1])
                        pe.wait_ge(gathered[k], GATH * (i + (EARLY_ITERS + 1)))
                        take(n, RING * i + (EARLY + k), k, pos % 2, lambda t: g[:, k, t, :])

            def alone(i):
                for j in range(RING):
                    pe.wait_ge(gathered[j], GATH * (i + (EARLY_ITERS + 1)))
                    take(RING * i + (A_UNITS - RING * A_ITERS + j), RING * i + (EARLY + j), j, j % 2,
                         lambda t: g[:, j, t, :])

            pe.wait_ge(acc_a_clear, 1)
            beside_early(0)
            with pe.Fori(1, A_ITERS) as i:
                beside_early(i)
            with pe.Fori(A_ITERS, REG_ITERS) as i:
                alone(i)

            pe.wait_ge(par_loaded, 16 * N_PARAMS)
            pe.wait_ge(added1, CHUNKS + 1)
            acc_cols = acc_a[:, 0:NODES].rearrange("f (p r) -> f r p", r=NR)
            for n in range(-(-NR // MID_R)):
                r0, r1 = n * MID_R, min(NR, n * MID_R + MID_R)
                for r in range(r0, r1):
                    k = (r - r0) * (FEAT + 1)
                    mm = pe.matmul(ps[:, n, k:k + FEAT + 1], acc_cols[0:FEAT + 1, r, :], w_l0_s[:, :],
                                   start=True, stop=True)
                mm.then_inc(mid_ready, 1)

            pe.wait_ge(table2_ready, 1)
            for n in range(-(-NR // 4)):
                wait(pe, turned_used, n - 1)
                for r in range(4 * n, min(NR, 4 * n + 4)):
                    k = (r - 4 * n) * P
                    mm = pe.transpose(ps[0:32, S_BANK + n % 2, k:k + P], hn[:, r, :], ident[:, :])
                mm.then_inc(turned, 1)

            def half(i, j, ahead):
                j, h = j + ahead // 2, ahead % 2
                return i + j // RING, j % RING, h

            def beyond(i, j, h):
                return isinstance(i, int) and i >= ITERS

            def hidden(i, j, h):
                if beyond(i, j, h):
                    return
                k = 2 * (RING * i + j) + h
                if h == 0:
                    pe.wait_ge(ef_in[j], 16 * (i + 1))
                wait(pe, hidden_ready, k - 1)
                pe.matmul(ps[0:HID, H_BANK + h, :], w1_s[32 * j:32 * j + 32, :],
                          ef[32 * j:32 * j + 32, 512 * h:512 * h + 512], start=True, stop=True,
                          tile_position=(32 * j, 0)).then_inc(hidden_psum, 1)

            def weights(i, j, h):
                if beyond(i, j, h):
                    return
                k = 2 * (RING * i + j) + h
                pe.wait_ge(hidden_ready, k + 1)
                wait(pe, weights_used, k - 1)
                for t in range(4):
                    mm = pe.matmul(w_ps[h][:, t, :], hid[:, h, P * t:P * t + P], w2_s[:, :], start=True, stop=True)
                mm.then_inc(weights_ready, 1)

            def messages_of(b):
                return [lambda t: prod_a[:, b, t, :], lambda t: msg_b[:, b, t, :]]

            def layer2(i):
                for j in range(RING):
                    c = RING * i + j
                    b = j % 2
                    hidden(*half(i, j, 3))
                    weights(*half(i, j, 2))
                    hidden(*half(i, j, 4))
                    weights(*half(i, j, 3))
                    if not (isinstance(c, int) and c == 0):
                        more_windows(c - 1, messages_of(1 - b), j, 1 - b, 1)
                    pe.wait_ge(messages_ready, c + 1)
                    wait(pe, added2, c - 1)
                    segment_sums(lambda t: onehot[:, b, t, :], messages_of(b), j, b, seg2_done, 1)

            hidden(0, 0, 0)
            hidden(0, 0, 1)
            pe.wait_ge(weights_scaled, 1)
            weights(0, 0, 0)
            hidden(0, 1, 0)
            weights(0, 0, 1)
            pe.wait_ge(turned_used, -(-NR // 4))
            over_iterations(pe, layer2)
            more_windows(CHUNKS - 1, messages_of((CHUNKS - 1) % 2), 0, (CHUNKS - 1) % 2, 1)

            pe.wait_ge(added2, CHUNKS + 1)
            accb_cols = acc_b[:, 0:NODES].rearrange("f (p r) -> f r p", r=NR)
            for n in range(-(-NR // FIN_R)):
                r0, r1 = n * FIN_R, min(NR, n * FIN_R + FIN_R)
                for r in range(r0, r1):
                    dest = ps[:, n, (r - r0) * FEAT:(r - r0 + 1) * FEAT]
                    pe.matmul(dest, acc_cols[:, r, :], sel_a_s[:, :], start=True, stop=False)
                    mm = pe.matmul(dest, accb_cols[0:96, r, :], sel_b_s[:, :], start=False, stop=True)
                mm.then_inc(fin_ready, 1)

        @block.vector
        def _(dve):
            extra = dve.alloc_register("dve_extra")
            copied = dve.alloc_register("dve_copied")
            dve.reg_mov(extra, 0)
            dve.reg_mov(copied, 0)
            chain = [0]

            def link(ins):
                chain[0] += 1
                ins.then_inc(dve_chain, 1)
                dve.wait_ge(dve_chain, chain[0])

            def rows(ap, n):
                return ap[:, :, None].to_broadcast([P, NR, n])

            def rsqrt(v, y):
                roots[0] += 1
                dve.sem_inc(root_asked, 1)
                dve.wait_ge(root_given, roots[0])
                t = stat[:, 0, :]
                link(dve.reciprocal(y, root[:, :]))
                link(dve.tensor_tensor(t, y, y, ALU.mult))
                link(dve.tensor_tensor(t, t, v, ALU.mult))
                link(dve.tensor_scalar(t, t, -0.5, 1.5, ALU.mult, ALU.add))
                link(dve.tensor_tensor(y, y, t, ALU.mult))

            roots = [0]

            def centre():
                link(dve.tensor_reduce(stat[:, 0, :], x[:, :, :], AX, ALU.add))
                link(dve.tensor_scalar(stat[:, 1, :], stat[:, 0, :], -1.0 / FEAT, None, ALU.mult))
                link(dve.tensor_tensor(xc[:, :, :], x[:, :, :], rows(stat[:, 1, :], FEAT), ALU.add))
                link(dve.tensor_tensor(hn[:, :, :], xc[:, :, :], xc[:, :, :], ALU.mult))
                link(dve.tensor_reduce(stat[:, 0, :], hn[:, :, :], AX, ALU.add))
                link(dve.tensor_scalar(stat[:, 1, :], stat[:, 0, :], 1.0 / FEAT, EPS, ALU.mult, ALU.add))
                rsqrt(stat[:, 1, :], stat[:, 2, :])

            dve.memset(w2_s[:, :], 0.0).then_inc(params_clear, 1)
            dve.memset(zero_b, 0.0).then_inc(zero_ready, 1)
            link(dve.memset(g[:, :, :, FEAT:FEAT + 1], 1.0))

            dve.wait_ge(x_loaded, 16)
            centre()
            dve.scalar_tensor_tensor(out=hn[:, :, :], in0=xc[:, :, :], scalar=0.0, in1=rows(stat[:, 2, :], FEAT),
                                     op0=ALU.max, op1=ALU.mult).then_inc(table0_ready, 1)

            dve.wait_ge(src_loaded, 16)
            link(dve.tensor_copy(src_f, src_i))
            link(dve.tensor_scalar(tmp, src_f, 1.0 / NR, -(NR - 1) / 2.0 / NR, ALU.mult, ALU.add))
            link(dve.tensor_scalar(tmp, tmp, RNE, -RNE, ALU.add, ALU.add))
            link(dve.tensor_copy(dig_p, tmp))
            link(dve.scalar_tensor_tensor(out=dig_r, in0=tmp, scalar=-float(NR), in1=src_f, op0=ALU.mult, op1=ALU.add))
            dve.wait_ge(iota_done, 4)

            def count(i):
                for b in range(2):
                    n = 2 * i + b
                    wait(dve, hist_used, n - 1)
                    for iota, dig, oh, m in ((iota_p, dig_p, oh_p, P), (iota_r, dig_r, oh_r, NR)):
                        ins = dve.tensor_tensor(oh[:, b, :, :], iota,
                                                dig[:, None, bass.ds(n * HB, HB)].to_broadcast([P, m, HB]),
                                                ALU.is_equal)
                    ins.then_inc(hist_ready, 1)

            count(0)
            with dve.Fori(1, HBATCH // 2) as i:
                count(i)

            dve.wait_ge(degrees_done, 1)
            link(dve.tensor_scalar(stat[:, 1, :], ps[:, H_BANK, 0:NR], 1.0, None, ALU.max))
            rsqrt(stat[:, 1, :], norm_src[:, :])
            dve.wait_ge(table0_ready, 1)
            dve.tensor_tensor(xc[:, :, :], hn[:, :, :], rows(norm_src[:, :], FEAT), ALU.mult).then_inc(table1_ready, 1)

            dve.wait_ge(dstc_loaded, 16)
            dve.tensor_reduce(mm_c[:, 0, :], dst_c[:, :, :], AX, ALU.min).then_inc(bounds_done, 1)
            dve.tensor_reduce(mm_c[:, 1, :], dst_c[:, :, :], AX, ALU.max).then_inc(bounds_done, 1)
            dve.wait_ge(dst_loaded, 16)
            link(dve.tensor_copy(dst_rel[:, :], dst_i))
            dve.memset(acc_a[:, :], 0.0).then_inc(acc_a_clear, 1)
            link(dve.tensor_scalar(part_rne[:, :], part_rne[:, :], RNE, None, ALU.add))
            link(dve.memset(early_g[:, :, FEAT:FEAT + 1], 1.0))
            dve.wait_ge(bounds_in, 32)
            link(dve.tensor_tensor(dst_rel[:, :].rearrange("p (c t) -> p c t", t=TILES),
                                   dst_rel[:, :].rearrange("p (c t) -> p c t", t=TILES),
                                   bound[:, 0, :, None].to_broadcast([P, CHUNKS, TILES]), ALU.subtract))
            link(dve.tensor_copy(row_i[:, 0, :], bound[0:1, 0, :]))
            link(dve.tensor_tensor(row_i[:, 1, :], bound[0:1, 1, :], bound[0:1, 0, :], ALU.subtract))

            def make_onehot(c, b, done):
                dve.tensor_tensor(onehot[:, b, :, :], iota_all[:, None, 0:WIN].to_broadcast([P, TILES, WIN]),
                                  dst_rel[:, bass.ds(c * TILES, TILES)][:, :, None].to_broadcast([P, TILES, WIN]),
                                  ALU.is_equal).then_inc(done, 1)

            def add_sums(at, b, layer, done):
                if layer == 0:
                    parts = [(acc_a, FEAT + 1, 0)]
                else:
                    parts = [(acc_a, P, 0), (acc_b, MW, 128)]
                for acc, m, col in parts:
                    here = acc[0:m, bass.ds(at, WIN)]
                    ins = dve.tensor_tensor(here, here, ps[0:m, S_BANK + b, col:col + WIN], ALU.add)
                ins.then_inc(done, 1)

            def bounds_of(c):
                return (dve.value_load(row_i[0:1, 0, bass.ds(c, 1)], min_val=0, max_val=NODES - 1),
                        dve.value_load(row_i[0:1, 1, bass.ds(c, 1)], min_val=0, max_val=NODES))

            def more_windows(c, b, base, span, layer):
                with dve.If(span > WIN - 1):
                    dve.reg_add(copied, copied, 1)
                    dve.tensor_copy(dst_x[:, :], dst_rel[:, bass.ds(c * TILES, TILES)]).then_inc(x_copied, 1)
                    with dve.Fori(WIN, span + 1, WIN) as off:
                        dve.wait_ge(x_copied, dve.snap(copied))
                        dve.reg_add(extra, extra, 1)
                        n = dve.snap(extra)
                        dve.tensor_scalar(dst_x[:, :], dst_x[:, :], -float(WIN), None, ALU.add).then_inc(x_shifted, 1)
                        dve.wait_ge(x_shifted, n)
                        dve.tensor_tensor(onehot_x[:, :, :], iota_all[:, None, 0:WIN].to_broadcast([P, TILES, WIN]),
                                          dst_x[:, :, None].to_broadcast([P, TILES, WIN]),
                                          ALU.is_equal).then_inc(x_onehot, 1)
                        dve.wait_ge(x_seg, n)
                        at = nc.s_assert_within(base + off, min_val=0, max_val=NODES - 1)
                        add_sums(at, b, layer, x_added)
                        dve.wait_ge(x_added, n)

            def early_onehots(e):
                dve.wait_ge(early_divided, e + 1)
                dve.tensor_scalar(early_p, early_div, RNE, part_rne[:, 0:1], ALU.add,
                                  ALU.is_equal).then_inc(early_p_ready, 1)
                dve.tensor_tensor(early_r, iota_all[:, None, :].to_broadcast([P, TILES, NR]),
                                  dig_r[:, bass.ds(e * TILES, TILES)][:, :, None].to_broadcast([P, TILES, NR]),
                                  ALU.is_equal).then_inc(early_r_ready, 1)

            def early_rows(e):
                dve.wait_ge(early_norm_psum, e + 1)
                dve.wait_ge(early_r_ready, e + 1)
                for b in range(2):
                    half = slice(4 * b, 4 * b + 4)
                    ins = dve.tensor_tensor(early_sel[:, half, :], early_r[:, half, :],
                                            ps[:, W_BANK + b, 0:4 * NR].rearrange("p (t r) -> p t r", r=NR), ALU.mult)
                ins.then_inc(early_chain, 1)
                dve.wait_ge(early_chain, 2 * e + 1)
                dve.tensor_reduce(early_norm, early_sel, AX, ALU.add).then_inc(early_chain, 1)
                dve.wait_ge(early_chain, 2 * e + 2)
                dve.wait_ge(kept, EARLY)
                dve.tensor_tensor(early_g[:, :, 0:FEAT],
                                  early[:, bass.ds(e * (TILES * FEAT), TILES * FEAT)].rearrange("p (t f) -> p t f", f=FEAT),
                                  early_norm[:, :, None].to_broadcast([P, TILES, FEAT]),
                                  ALU.mult).then_inc(early_g_ready, 1)

            def take(n, c, b):
                base, span = bounds_of(c)
                dve.wait_ge(seg1_done, n + 1)
                wait(dve, added1, n)
                add_sums(base, b, 0, added1)
                more_windows(c, b, base, span, 0)

            def beside_early(i):
                for pos, (is_early, k) in enumerate(UNITS):
                    nxt_i, nxt_pos = (i, pos + 1) if pos + 1 < len(UNITS) else (i + 1, 0)
                    nxt_early, nxt_k = UNITS[nxt_pos]
                    if nxt_early:
                        early_onehots(2 * i + nxt_k)
                    make_onehot(2 * i + nxt_k if nxt_early else RING * nxt_i + (EARLY + nxt_k),
                                1 - pos % 2, onehot1_ready)
                    if is_early:
                        early_rows(2 * i + k)
                    take(len(UNITS) * i + pos, 2 * i + k if is_early else RING * i + (EARLY + k), pos % 2)

            def alone(i):
                for j in range(RING):
                    if not (isinstance(i, int) and j == RING - 1):
                        make_onehot(RING * i + (EARLY + j + 1), 1 - j % 2, onehot1_ready)
                    take(RING * i + (A_UNITS - RING * A_ITERS + j), RING * i + (EARLY + j), j % 2)

            early_r_ready, early_chain = sem("early_r_ready"), sem("early_chain")
            make_onehot(EARLY, 0, onehot1_ready)
            beside_early(0)
            with dve.Fori(1, A_ITERS) as i:
                beside_early(i)
            with dve.Fori(A_ITERS, REG_ITERS - 1) as i:
                alone(i)
            alone(REG_ITERS - 1)
            dve.wait_ge(added1, CHUNKS)
            dve.memset(stat[:, 0, 0:1], 0.0).then_inc(added1, 1)

            dve.wait_ge(table1_out, 16)
            dve.wait_ge(par_loaded, 16 * N_PARAMS)
            def mid_bank(n):
                r0, r1 = n * MID_R, min(NR, n * MID_R + MID_R)
                return r0, r1, ps[:, n, 0:(r1 - r0) * (FEAT + 1)].rearrange("p (r f) -> p r f", f=FEAT + 1)

            for n in range(-(-NR // MID_R)):
                r0, r1, z = mid_bank(n)
                dve.wait_ge(mid_ready, n + 1)
                link(dve.tensor_scalar(stat[:, 1, r0:r1], z[:, :, FEAT], 1.0, None, ALU.max))
            rsqrt(stat[:, 1, :], stat[:, 3, :])
            for n in range(-(-NR // MID_R)):
                r0, r1, z = mid_bank(n)
                link(dve.tensor_tensor(xc[:, r0:r1, :], z[:, :, 0:FEAT],
                                       stat[:, 3, r0:r1, None].to_broadcast([P, r1 - r0, FEAT]), ALU.mult))
            link(dve.tensor_tensor(xc[:, :, :], xc[:, :, :], b_l0_s[:, None, :].to_broadcast([P, NR, FEAT]), ALU.add))
            link(dve.scalar_tensor_tensor(out=x[:, :, :], in0=xc[:, :, :], scalar=0.0, in1=x[:, :, :],
                                          op0=ALU.max, op1=ALU.add))
            dve.wait_ge(table0_out, 16)
            centre()
            link(dve.scalar_tensor_tensor(out=hn[:, :, 0:MUL], in0=xc[:, :, 0:MUL], scalar=0.0,
                                          in1=rows(stat[:, 2, :], MUL), op0=ALU.max, op1=ALU.mult))
            for m in range(3):
                ins = dve.scalar_tensor_tensor(
                    out=hn[:, :, MUL + MUL * m:MUL + MUL * m + MUL], in0=xc[:, :, MUL + m:FEAT:3], scalar=0.0,
                    in1=rows(stat[:, 2, :], MUL), op0=ALU.max, op1=ALU.mult)
            ins.then_inc(table2_ready, 1)
            link(dve.memset(acc_a[:, :], 0.0))
            link(dve.tensor_scalar(w2_s[:, 0:64], w2_s[:, 0:64], float(ALPHA * C110), None, ALU.mult))
            link(dve.tensor_scalar(w2_s[:, 64:256], w2_s[:, 64:256], float(ALPHA), None, ALU.mult))
            dve.tensor_scalar(sel_b_s[64:96, :], sel_b_s[64:96, :], float(SI_SCALE), None,
                              ALU.mult).then_inc(weights_scaled, 1)

            def d_coefs(i, j):
                c = RING * i + j
                b = j % 2
                make_onehot(c, b, x_dummy)
                dve.wait_ge(coefs_ready, c + 1)
                dve.tensor_tensor(vsh[:, :, :, :], g[:, j, :, MUL:FEAT].rearrange("p t (m i) -> p t i m", m=3),
                                  sh[:, j, :, None, 1:4].to_broadcast([P, TILES, MUL, 3]),
                                  ALU.mult).then_inc(vsh_ready, 1)
                dve.wait_ge(vsh_ready, c + 1)
                dve.tensor_reduce(q[:, b, :, 0:MUL], vsh[:, :, :, :], AX, ALU.add).then_inc(d_ready, 1)

            x_dummy = sem("onehot2_ready")

            def products(c, j, h):
                k = 2 * c + h
                b = j % 2
                w = w_ps[h]
                qt = q[:, b, 4 * h:4 * h + 4, :]
                dve.wait_ge(weights_ready, k + 1)
                dve.tensor_tensor(
                    prod_b[:, h, :, 0:3, :].rearrange("p t m (i o) -> p t m i o", o=MUL),
                    w[:, :, 128:192].rearrange("p t (i o) -> p t i o", o=MUL)[:, :, None, :, :].to_broadcast([P, 4, 3, MUL, MUL]),
                    qt[:, :, 16:40].rearrange("p t (m i) -> p t m i", m=3)[:, :, :, :, None].to_broadcast([P, 4, 3, MUL, MUL]),
                    ALU.mult)
                dve.tensor_tensor(
                    prod_b[:, h, :, 3, :].rearrange("p t (i o) -> p t i o", o=MUL),
                    w[:, :, 192:256].rearrange("p t (i o) -> p t i o", o=MUL),
                    qt[:, :, 40:48, None].to_broadcast([P, 4, MUL, MUL]), ALU.mult).then_inc(prodb_ready, 1)
                if h == 0:
                    dve.wait_ge(d_ready, c + 1)
                dve.tensor_tensor(
                    prod_a[:, b, 4 * h:4 * h + 4, :].rearrange("p t (k o) -> p t k o", o=MUL),
                    w[:, :, 0:128].rearrange("p t (k o) -> p t k o", o=MUL),
                    qt[:, :, 0:16, None].to_broadcast([P, 4, 16, MUL]), ALU.mult).then_inc(weights_used, 1)
                dve.wait_ge(prodb_ready, k + 1)
                dve.tensor_reduce(
                    msg_b[:, b, 4 * h:4 * h + 4, 0:32].rearrange("p t (g o) -> p t g o", o=MUL),
                    prod_b[:, h, :, :, :].rearrange("p t g (i o) -> p t g o i", o=MUL),
                    AX, ALU.add).then_inc(reduced, 1)

            def finish_messages(c, j):
                b = j % 2
                dve.wait_ge(reduced, 2 * c + 2)
                dve.tensor_tensor(
                    msg_b[:, b, :, 32:56].rearrange("p t (m o) -> p t m o", m=3),
                    msg_b[:, b, :, None, 24:32].to_broadcast([P, TILES, 3, MUL]),
                    sh[:, j, :, 1:4, None].to_broadcast([P, TILES, 3, MUL]), ALU.mult).then_inc(messages_ready, 1)

            def join_sums(c, b, base, span):
                dve.wait_ge(seg2_done, c + 1)
                wait(dve, added2, c)
                add_sums(base, b, 1, added2)
                more_windows(c, b, base, span, 1)

            def layer2(i):
                for j in range(RING):
                    c = RING * i + j
                    b = j % 2
                    first = isinstance(c, int) and c == 0
                    if not first:
                        limits = bounds_of(c - 1)
                    products(c, j, 1)
                    if not first:
                        join_sums(c - 1, 1 - b, *limits)
                    finish_messages(c, j)
                    if not (isinstance(c, int) and c == CHUNKS - 1):
                        nxt = (i, j + 1) if j + 1 < RING else (i + 1, 0)
                        d_coefs(*nxt)
                        products(c + 1, nxt[1], 0)

            d_coefs(0, 0)
            products(0, 0, 0)
            over_iterations(dve, layer2)
            join_sums(CHUNKS - 1, (CHUNKS - 1) % 2, *bounds_of(CHUNKS - 1))
            dve.wait_ge(added2, CHUNKS)
            dve.memset(stat[:, 0, 0:1], 0.0).then_inc(added2, 1)

            for n in range(-(-NR // FIN_R)):
                r0, r1 = n * FIN_R, min(NR, n * FIN_R + FIN_R)
                dve.wait_ge(fin_ready, n + 1)
                dve.tensor_tensor(xc[:, r0:r1, :], x[:, r0:r1, :],
                                  ps[:, n, 0:(r1 - r0) * FEAT].rearrange("p (r f) -> p r f", f=FEAT),
                                  ALU.add).then_inc(out_ready, 1)


def selections():
    a = np.zeros((P, FEAT), np.float32)
    b = np.zeros((64, FEAT), np.float32)
    for o in range(MUL):
        a[o::MUL, o] = 1.0
        for m in range(3):
            b[m * MUL + o, MUL + 3 * o + m] = 1.0
            b[32 + m * MUL + o, MUL + 3 * o + m] = 1.0
    return a, b


def kernel(x, src, dst, edge_attr_32, edge_attr_4, L0_gnn_weight, L0_gnn_bias, L1_gnn_W1, L1_gnn_b1,
           L1_gnn_W2, L1_gnn_b2, L1_gnn_si_w0, L1_gnn_si_w1):
    import concourse.bacc as bacc
    from concourse.bass_utils import run_bass_kernel_spmd

    edges = CHUNKS * CHUNK
    pad = edges - N_EDGES
    xn = np.pad(np.asarray(x), ((0, NODES - N_NODES), (0, 0))).reshape(P, NR * FEAT)
    s = np.pad(np.asarray(src), (0, pad), constant_values=NODES - 1)
    d = np.pad(np.asarray(dst), (0, pad), constant_values=N_NODES)
    ea = np.pad(np.asarray(edge_attr_32), ((0, pad), (0, 0))).reshape(CHUNKS, CHUNK, FEAT).transpose(0, 2, 1)
    e4 = np.pad(np.asarray(edge_attr_4), ((0, pad), (0, 0))).reshape(CHUNKS, TILES, P, 4).transpose(0, 2, 1, 3)
    w0 = np.zeros((FEAT + 1, FEAT + 1), np.float32)
    w0[:FEAT, :FEAT] = L0_gnn_weight
    w0[FEAT, FEAT] = 1.0
    mm = MUL * MUL
    w2 = np.concatenate([np.asarray(L1_gnn_W2), np.asarray(L1_gnn_b2)[None, :]])
    w2 = np.concatenate([w2[:, 3 * mm:], w2[:, :mm], w2[:, 2 * mm:3 * mm], w2[:, mm:2 * mm]], axis=1)
    skip = np.zeros((FEAT, FEAT), np.float32)
    skip[:MUL, :MUL] = L1_gnn_si_w0
    for m in range(3):
        skip[MUL + MUL * m:MUL + MUL * m + MUL, MUL + m::3] = L1_gnn_si_w1
    sel_a, sel_b = selections()
    arrays = {
        "x_nodes": xn,
        "src_all": s.reshape(CHUNKS * TILES, P).T,
        "src_chunks": s.reshape(CHUNKS, TILES, P).transpose(0, 2, 1),
        "src_rows": s.reshape(CHUNKS, CHUNK),
        "dst_all": d.reshape(CHUNKS * TILES, P).T,
        "dst_chunks": d.reshape(CHUNKS, CHUNK),
        "edge_t": ea,
        "sh_chunks": e4.reshape(CHUNKS, P, TILES * 4),
        "w_l0": w0,
        "b_l0": np.asarray(L0_gnn_bias)[None, :],
        "w1": np.asarray(L1_gnn_W1),
        "b1": np.asarray(L1_gnn_b1)[:, None],
        "w2": w2,
        "skip_w": skip,
        "sel_a": sel_a,
        "sel_b": sel_b,
        "ident_in": np.eye(P, dtype=np.float32),
    }
    arrays = {k: np.ascontiguousarray(v) for k, v in arrays.items()}
    nc = bacc.Bacc("TRN2", target_bir_lowering=False, num_devices=1)
    aps = {k: nc.dram_tensor(k, v.shape, mybir.dt.from_np(v.dtype), kind="ExternalInput").ap()
           for k, v in arrays.items()}
    out = nc.dram_tensor("out", (NODES, FEAT), F32, kind="ExternalOutput").ap()
    gnn_program(nc, **aps, out=out)
    r = run_bass_kernel_spmd(nc, [arrays], core_ids=[0])
    return r.results[0]["out"][:N_NODES]
```

```python
from contextlib import ExitStack

import numpy as np
import concourse.bass as bass
from concourse import mybir

ALU = mybir.AluOpType
ACT = mybir.ActivationFunctionType
F32 = mybir.dt.float32
BF16 = mybir.dt.bfloat16
I32 = mybir.dt.int32
AX = mybir.AxisListType.X

P = 128
N_NODES, N_EDGES = 12500, 212500
FEAT, HID, MUL = 32, 64, 8
BR = 4
BLOCK = P * BR
BLOCKS = -(-N_NODES // BLOCK)
NR = BLOCKS * BR
NODES = P * NR
BR_LOG, BLOCK_LOG = BR.bit_length() - 1, BLOCK.bit_length() - 1
TILES = 8
CHUNK = TILES * P
RING = 4
CHUNKS = -(-N_EDGES // (CHUNK * RING)) * RING
ITERS = CHUNKS // RING
WIN = 68
ACC_W = NODES + WIN
EARLY = 32
EARLY_ITERS = EARLY // RING
A_ITERS = EARLY // 2
A_UNITS = A_ITERS * (RING + 2)
REG_ITERS = ITERS - EARLY_ITERS
UNITS = ((0, 0), (0, 1), (1, 0), (0, 2), (0, 3), (1, 1))
LOOK = 1
N_PARAMS = 8 + RING
EPS = 1e-5
ALPHA, C110, SI_SCALE = 0.25, 1.0 / np.sqrt(3.0), 1.0 / np.sqrt(float(MUL))
HB = 16
HBATCH = CHUNKS * TILES // HB
EARLY_LINKS = 6
MID_LINKS = 24
MW = 56


def gnn_program(nc, x_rows, src_all, src_chunks, src_rows, dst_all, dst_chunks, edge_t, sh_chunks,
                w_l0, b_l0, w1, b1, w2, skip_w, sel_a, sel_b, ident_in, out):
    assert EARLY % RING == 0 and REG_ITERS > A_ITERS + 1
    assert CHUNKS % (2 * HB // TILES) == 0 and CHUNKS % 2 == 0
    with ExitStack() as ctx:
        def sb(name, shape, dt=F32):
            return ctx.enter_context(nc.sbuf_tensor(name, shape, dt))

        def sem(name):
            return ctx.enter_context(nc.semaphore(name))

        table1 = nc.dram_tensor("table1", [NODES, FEAT], F32).ap()
        table2 = nc.dram_tensor("table2", [NODES, FEAT], F32).ap()
        bounds = nc.dram_tensor("bounds", [2, CHUNKS], F32).ap()

        ps = ctx.enter_context(nc.psum_tensor("ps", [P, 8, 512], F32))
        W_BANK, H_BANK, S_BANK = 0, 4, 6

        acc_a = sb("acc_a", [P, ACC_W])
        acc_b = sb("acc_b", [P, ACC_W])
        x = sb("x", [P, NR, FEAT])
        xc = sb("xc", [P, NR, FEAT])
        hn = sb("hn", [P, NR, FEAT])
        stat = sb("stat", [P, 4, NR])
        norm_src = sb("norm_src", [P, NR])
        root = sb("root", [P, NR])
        dst_rel = sb("dst_rel", [P, CHUNKS * TILES])
        bound = sb("bound", [P, 2, CHUNKS])
        row_i = sb("row_i", [1, 3, CHUNKS], I32)
        mm_c = sb("mm_c", [CHUNKS // 2, 2, 2])
        iota_all = sb("iota_all", [P, P])
        part = sb("part", [P, 1])
        idx = sb("idx", [P, RING, TILES], I32)
        g = sb("g", [P, RING, TILES, FEAT + 1])
        sh = sb("sh", [P, RING, TILES, 4])
        onehot = sb("onehot", [P, 2, TILES, WIN])
        onehot_x = sb("onehot_x", [P, TILES, WIN])
        dst_x = sb("dst_x", [P, TILES])
        ef = sb("ef", [P, CHUNK])
        hid = sb("hid", [P, 2, 512])
        q = sb("q", [P, 2, TILES, 48])
        vsh = sb("vsh", [P, TILES, MUL, 3])
        prod_a = sb("prod_a", [P, 2, TILES, 128])
        prod_b = sb("prod_b", [P, 2, 4, 4, 64])
        msg_b = sb("msg_b", [P, 2, TILES, MW])
        ident = sb("ident", [P, P])
        w_l0_s = sb("w_l0_s", [FEAT + 1, FEAT + 1])
        b_l0_s = sb("b_l0_s", [P, FEAT])
        w1_s = sb("w1_s", [P, HID])
        b1_s = sb("b1_s", [HID, 1])
        w2_s = sb("w2_s", [P, 4 * MUL * MUL])
        sel_a_s = sb("sel_a_s", [P, FEAT])
        sel_b_s = sb("sel_b_s", [96, FEAT])

        hist = acc_b[:, :].bitcast(BF16)
        T_ALL = CHUNKS * TILES
        o = 0
        dig_p = msg_b[:, :, :, :].rearrange("p b t k -> p (b t k)").bitcast(BF16)[:, 0:T_ALL]
        dig_r, o = hist[:, o:o + T_ALL], o + T_ALL
        oh_p, o = hist[:, o:o + 2 * P * HB].rearrange("p (b j t) -> p b j t", b=2, t=HB), o + 2 * P * HB
        oh_r, o = hist[:, o:o + 2 * NR * HB].rearrange("p (b j t) -> p b j t", b=2, t=HB), o + 2 * NR * HB
        zero_b, o = hist[:, o:o + P], o + P
        early_at = -(-o // 2)
        early = acc_b[:, early_at:early_at + EARLY * TILES * FEAT]
        assert early_at + EARLY * TILES * FEAT <= ACC_W
        iotas = prod_a[:, :, :, :].rearrange("p b t k -> p (b t k)").bitcast(BF16)
        iota_p = iotas[:, 0:P * HB].rearrange("p (j t) -> p j t", t=HB)
        iota_r = iotas[:, P * HB:(P + NR) * HB].rearrange("p (j t) -> p j t", t=HB)
        dst_i, src_i, src_p, src_b, src_r = (acc_a[:, k * T_ALL:(k + 1) * T_ALL].bitcast(I32) for k in range(5))
        flat_b = prod_b[:, :, :, :, :].rearrange("p h t g k -> p (h t g k)")
        dst_c = flat_b[0:CHUNKS // 2, 0:2 * CHUNK].bitcast(I32).rearrange("q (s e) -> q s e", s=2)
        early_src = ef[:, :].bitcast(I32)
        early_digit = flat_b[:, 0:CHUNK].bitcast(I32)
        early_sel = flat_b[:, CHUNK:CHUNK + TILES * NR].rearrange("p (t r) -> p t r", r=NR)
        early_p = hid[:, :, :].rearrange("p b e -> p (b e)")
        early_r_all = msg_b[:, :, :, :].rearrange("p b t k -> p (b t k)")
        early_r = early_r_all[:, 0:TILES * NR].rearrange("p (t r) -> p t r", r=NR)
        flat_q = q[:, :, :, :].rearrange("p b t k -> p (b t k)")
        early_g = flat_q[:, 0:TILES * (FEAT + 1)].rearrange("p (t f) -> p t f", f=FEAT + 1)
        later_w = 2 * CHUNKS
        later = early_r_all[0:1, 0:2 * later_w].rearrange("a (b c) -> a b c", b=2)
        early_norm = flat_q[:, TILES * (FEAT + 1):TILES * (FEAT + 2)]
        early_mean = flat_q[:, TILES * (FEAT + 2):TILES * (FEAT + 3)]
        early_x = flat_q[:, TILES * (FEAT + 3):TILES * (2 * FEAT + 3)].rearrange("p (t f) -> p t f", f=FEAT)

        src_loaded, dst_loaded, dstc_loaded, x_loaded, par_loaded = (
            sem(n) for n in ("src_loaded", "dst_loaded", "dstc_loaded", "x_loaded", "par_loaded"))
        bounds_done, bounds_out, bounds_in = sem("bounds_done"), sem("bounds_out"), sem("bounds_in")
        iota_done = sem("iota_done")
        hist_ready, hist_used, degrees_done = sem("hist_ready"), sem("hist_used"), sem("degrees_done")
        dve_chain = sem("dve_chain")
        params_clear = sem("params_clear")
        zero_ready, acc_a_clear, weights_scaled = sem("zero_ready"), sem("acc_a_clear"), sem("weights_scaled")
        kept = sem("kept")
        early_src_in, early_digits = sem("early_src_in"), sem("early_digits")
        early_p_ready, early_norm_psum, early_g_ready = (
            sem("early_p_ready"), sem("early_norm_psum"), sem("early_g_ready"))
        table1_ready, table1_out = sem("table1_ready"), sem("table1_out")
        table2_ready, table2_out = sem("table2_ready"), sem("table2_out")
        idx_in = [sem(f"idx_in{j}") for j in range(RING)]
        sh_in = [sem(f"sh_in{j}") for j in range(RING)]
        ef_in = [sem(f"ef_in{j}") for j in range(RING)]
        gathered = [sem(f"gathered{j}") for j in range(RING)]
        onehot1_ready, seg1_done, added1 = sem("onehot1_ready"), sem("seg1_done"), sem("added1")
        mid_ready = sem("mid_ready")
        hidden_psum, hidden_ready = sem("hidden_psum"), sem("hidden_ready")
        weights_ready, weights_used = sem("weights_ready"), sem("weights_used")
        coefs_ready, vsh_ready, d_ready = sem("coefs_ready"), sem("vsh_ready"), sem("d_ready")
        prodb_ready, reduced, messages_ready = sem("prodb_ready"), sem("reduced"), sem("messages_ready")
        seg2_done, added2 = sem("seg2_done"), sem("added2")
        turned, turned_used = sem("turned"), sem("turned_used")
        acc_b_clear = sem("acc_b_clear")
        slots_opened = sem("slots_opened")
        root_asked, root_given = sem("root_asked"), sem("root_given")
        x_copied, x_shifted, x_onehot, x_seg, x_added = (
            sem(n) for n in ("x_copied", "x_shifted", "x_onehot", "x_seg", "x_added"))
        rows_ready = sem("rows_ready")
        mid_go, mid_chain, fin_go = sem("mid_go"), sem("mid_chain"), sem("fin_go")
        sums_there = sem("sums_there")
        fin_ready, out_ready, out_stored = sem("fin_ready"), sem("out_ready"), sem("out_stored")

        def by_block(dram):
            return dram.rearrange("(b p r) f -> p b r f", p=P, r=BR)

        def blocks_of(tile):
            return tile[:, :, :].rearrange("p (b r) f -> p b r f", r=BR)

        def wait(eng, s, value):
            if not isinstance(value, int) or value > 0:
                eng.wait_ge(s, value)

        def over_iterations(eng, body):
            body(0)
            with eng.Fori(1, ITERS - 1) as i:
                body(i)
            body(ITERS - 1)

        def final_blocks(eng, c):
            return eng.value_load(row_i[0:1, 2, bass.ds(c, 1)], min_val=0, max_val=BLOCKS - 1)

        def next_block(eng, done, final, finish):
            with eng.If(final > eng.snap(done, min_val=0, max_val=BLOCKS)):
                finish(eng.snap(done, min_val=0, max_val=BLOCKS - 1))
                eng.reg_add(done, done, 1)

        def other_blocks(eng, done, finish):
            with eng.Fori(eng.snap(done, min_val=0, max_val=BLOCKS - 1), BLOCKS) as b:
                finish(nc.s_assert_within(b, min_val=0, max_val=BLOCKS - 1))

        def counter(eng, name):
            reg = eng.alloc_register(name)
            eng.reg_mov(reg, 0)
            return reg

        def by_column(staged):
            return staged.rearrange("f (p r) -> f r p", r=BR)

        def block_rows(dram, b):
            return by_block(dram)[:, bass.ds(b, 1), :, :].rearrange("p b r f -> p (b r) f")

        def block_columns(tile, b):
            return tile[:, bass.ds(b * BR, BR), :]

        assert BLOCK <= CHUNK and 2 * BLOCK <= NR * FEAT
        staged1 = ef[0:FEAT + 1, 0:BLOCK]
        flat_hn = hn[:, :, :].rearrange("p r f -> p (r f)")
        staged2 = [flat_hn[:, 0:BLOCK], flat_hn[0:96, BLOCK:2 * BLOCK]]
        mid_ps = ps[:, W_BANK, 0:BR * (FEAT + 1)].rearrange("p (r f) -> p r f", f=FEAT + 1)
        fin_ps = ps[:, S_BANK, 256:256 + BR * FEAT].rearrange("p (r f) -> p r f", f=FEAT)

        GATH = 16 * TILES
        w_ps = [ps[:, W_BANK + 2 * b:W_BANK + 2 * b + 2, :].rearrange("p b (u w) -> p (b u) w", w=256)
                for b in range(2)]
        block = ctx.enter_context(nc.Block())

        @block.sync
        def _(sp):
            for j in range(RING):
                sp.dma_start(idx[:, j, :], src_chunks[j]).then_inc(idx_in[j], 16)
                if j == 0:
                    sp.dma_start(blocks_of(x), by_block(x_rows)).then_inc(x_loaded, 16)
            sp.dma_start(src_i, src_all).then_inc(src_loaded, 16)
            sp.dma_start(dst_c, dst_chunks.rearrange("(q s) e -> q s e", s=2)).then_inc(dstc_loaded, 16)
            sp.dma_start(dst_i, dst_all).then_inc(dst_loaded, 16)
            sp.dma_start(w_l0_s[:, :], w_l0).then_inc(par_loaded, 16)
            sp.dma_start(b_l0_s[:, :], b_l0.to_broadcast([P, FEAT])).then_inc(par_loaded, 16)
            for j in range(RING):
                sp.dma_start(w1_s[32 * j:32 * j + 32, :], w1).then_inc(par_loaded, 16)
            sp.dma_start(b1_s[:, :], b1).then_inc(par_loaded, 16)
            sp.wait_ge(params_clear, 1)
            sp.dma_start(w2_s[0:HID + 1, :], w2).then_inc(par_loaded, 16)
            sp.dma_start(sel_a_s[:, :], sel_a).then_inc(par_loaded, 16)
            sp.dma_start(sel_b_s[0:64, :], sel_b).then_inc(par_loaded, 16)
            sp.dma_start(sel_b_s[64:96, :], skip_w).then_inc(par_loaded, 16)
            sp.dma_start(ident[:, :], ident_in).then_inc(par_loaded, 16)
            def load1(i):
                for j in range(RING):
                    sp.wait_ge(gathered[j], GATH * (i + 1))
                    sp.dma_start(idx[:, j, :], load_from(src_chunks, RING * i + RING + j)).then_inc(idx_in[j], 16)

            def load_from(dram, c):
                return dram[c] if isinstance(c, int) else dram[bass.ds(c, 1)].rearrange("a p k -> (a p) k")

            with sp.Fori(0, EARLY_ITERS - 1) as i:
                load1(i)
            sp.dma_start(early_src, src_rows[0:1, :].to_broadcast([P, CHUNK])).then_inc(early_src_in, 16)
            sp.wait_ge(bounds_done, 2)
            for k in range(2):
                sp.dma_start(bounds[k:k + 1, :].rearrange("a (q s) -> (a q) s", s=2), mm_c[:, k, :]).then_inc(bounds_out, 16)
            sp.wait_ge(bounds_out, 32)
            for k in range(2):
                sp.dma_start(bound[:, k, :], bounds[k:k + 1, :].to_broadcast([P, CHUNKS])).then_inc(bounds_in, 16)
            with sp.Fori(EARLY_ITERS - 1, ITERS - 1) as i:
                load1(i)
            for j in range(RING):
                sp.wait_ge(gathered[j], GATH * ITERS)
                sp.dma_start(idx[:, j, :], src_chunks[j]).then_inc(idx_in[j], 16)
                sp.dma_start(sh[:, j, :, :], sh_chunks[j].rearrange("p (t d) -> p t d", d=4)).then_inc(sh_in[j], 16)
            sp.wait_ge(mid_ready, BLOCKS)
            for j in range(RING):
                sp.dma_start(ef[32 * j:32 * j + 32, :], edge_t[j]).then_inc(ef_in[j], 16)
            sp.wait_ge(rows_ready, 1)
            blocks2 = counter(sp, "sp_blocks2")

            def store(b):
                sp.wait_ge(out_ready, b + 1)
                sp.dma_start(block_rows(out, b), block_columns(xc, b)).then_inc(out_stored, 16)

            with sp.Fori(0, ITERS - 1) as i:
                final = final_blocks(sp, RING * i + (LOOK - 1))
                for j in range(RING):
                    c = RING * i + j
                    sp.wait_ge(hidden_psum, 2 * c + 2)
                    sp.dma_start(ef[32 * j:32 * j + 32, :], load_from(edge_t, c + RING)).then_inc(ef_in[j], 16)
                    sp.wait_ge(gathered[j], GATH * (i + ITERS + 1))
                    sp.dma_start(idx[:, j, :], load_from(src_chunks, c + RING)).then_inc(idx_in[j], 16)
                    sp.wait_ge(messages_ready, c + 1)
                    sp.dma_start(sh[:, j, :, :].rearrange("p t d -> p (t d)"),
                                 load_from(sh_chunks, c + RING)).then_inc(sh_in[j], 16)
                next_block(sp, blocks2, final, store)
            next_block(sp, blocks2, final_blocks(sp, RING * (ITERS - 1) + (LOOK - 1)), store)
            other_blocks(sp, blocks2, store)
            sp.wait_ge(out_stored, 16 * BLOCKS)

        @block.gpsimd
        def _(pool):
            pool.iota(iota_all[:, :], [[1, P]], base=0, channel_multiplier=0,
                      allow_small_or_imprecise_dtypes=True).then_inc(iota_done, 1)
            pool.iota(part[:, :], [[1, 1]], base=0, channel_multiplier=1,
                      allow_small_or_imprecise_dtypes=True).then_inc(iota_done, 1)

            def gather(i, table, iteration, free):
                for j in range(RING):
                    pool.wait_ge(idx_in[j], 16 * (iteration + 1))
                    free(RING * i + j, j)
                    pool.sem_inc(slots_opened, 1)
                    for t in range(TILES):
                        pool.indirect_dma_start(
                            out=g[:, j, t, 0:FEAT], out_offset=None, in_=table,
                            in_offset=bass.IndirectOffsetOnAxis(ap=idx[:, j, t:t + 1], axis=0),
                        ).then_inc(gathered[j], 16)

            def kept_four_before(c, j):
                wait(pool, kept, c - RING + 1)

            def used_in(first_unit, per_iteration, position):
                def free(i):
                    return lambda c, j: pool.wait_ge(
                        onehot1_ready, first_unit + per_iteration * i + position[j] + 3)
                return free

            gather(0, x_rows, 0, kept_four_before)
            with pool.Fori(1, EARLY_ITERS) as i:
                gather(i, x_rows, i, kept_four_before)
            pool.wait_ge(table1_out, 16)
            gather(EARLY_ITERS, table1, EARLY_ITERS, kept_four_before)
            beside = used_in(0, len(UNITS), [UNITS.index((0, j)) for j in range(RING)])
            alone = used_in(A_UNITS, RING, range(RING))
            with pool.Fori(0, A_ITERS) as i:
                gather(i, table1, i + (EARLY_ITERS + 1), beside(i))
            with pool.Fori(0, REG_ITERS - A_ITERS - 1) as i:
                gather(i, table1, i + (EARLY_ITERS + 1 + A_ITERS), alone(i))

            pool.wait_ge(added1, A_UNITS)
            pool.memset(acc_b[:, :], 0.0).then_inc(acc_b_clear, 1)
            pool.wait_ge(acc_b_clear, 1)
            pool.memset(hid[HID:P, :, :], 0.0).then_inc(acc_b_clear, 1)
            pool.wait_ge(acc_b_clear, 2)
            pool.memset(hid[HID:HID + 1, :, :], 1.0).then_inc(acc_b_clear, 1)

            pool.wait_ge(table2_out, 16 * BLOCKS)
            over_iterations(pool, lambda i: gather(
                i, table2, i + ITERS, lambda c, j: wait(pool, d_ready, c - RING + 1)))

        @block.scalar
        def _(act):
            def square_root(n):
                act.wait_ge(root_asked, n)
                act.activation(root[:, :], stat[:, 1, :], ACT.Sqrt).then_inc(root_given, 1)

            def keep(i):
                for j in range(RING):
                    act.wait_ge(gathered[j], GATH * (i + 1))
                    dest = early[:, bass.ds((RING * i + j) * (TILES * FEAT), TILES * FEAT)]
                    act.activation(dest.rearrange("p (t f) -> p t f", f=FEAT), g[:, j, :, 0:FEAT],
                                   ACT.Copy).then_inc(kept, 1)

            square_root(1)
            with act.Fori(0, EARLY_ITERS - 1) as i:
                keep(i)
            square_root(2)
            act.wait_ge(table1_ready, 1)
            act.dma_start(by_block(table1), blocks_of(hn)).then_inc(table1_out, 16)
            keep(EARLY_ITERS - 1)

            def next_sources(e):
                act.wait_ge(early_digits, e + 1)
                row = src_rows[e + 1:e + 2, :] if isinstance(e, int) else src_rows[bass.ds(e + 1, 1), :]
                act.dma_start(early_src, row.to_broadcast([P, CHUNK])).then_inc(early_src_in, 16)

            with act.Fori(0, EARLY - 1) as e:
                next_sources(e)
            def mid_block(b):
                for k in range(2):
                    act.wait_ge(root_asked, 2 * b + (3 + k))
                    act.activation(root[:, 0:BR], stat[:, 1, 0:BR], ACT.Sqrt).then_inc(root_given, 1)
                act.wait_ge(table2_ready, b + 1)
                act.dma_start(block_rows(table2, b), block_columns(hn, b)).then_inc(table2_out, 16)

            act.wait_ge(rows_ready, 1)
            blocks1 = counter(act, "act_blocks1")
            with act.Fori(A_ITERS, REG_ITERS) as i:
                next_block(act, blocks1, final_blocks(act, RING * i + (EARLY + LOOK)), mid_block)
            other_blocks(act, blocks1, mid_block)
            act.wait_ge(acc_b_clear, 1)
            for n in range(-(-NR // 4)):
                k = min(4, NR - 4 * n)
                act.wait_ge(turned, n + 1)
                dest = acc_b[64:96, bass.ds(4 * n // BR * BLOCK, BLOCK)].rearrange(
                    "f (p r) -> f r p", r=BR)[:, 4 * n % BR:4 * n % BR + k, :]
                act.activation(dest, ps[0:32, S_BANK + n % 2, 0:128 * k].rearrange("f (r p) -> f r p", p=P),
                               ACT.Copy).then_inc(turned_used, 1)

            def relu(i, j, h):
                if isinstance(i, int) and i >= ITERS:
                    return
                act.wait_ge(hidden_psum, 2 * (RING * i + j) + h + 1)
                act.activation(hid[0:HID, h, :], ps[0:HID, H_BANK + h, :], ACT.Relu,
                               bias=b1_s[:, 0:1]).then_inc(hidden_ready, 1)

            def coefs(i, j):
                if isinstance(i, int) and i >= ITERS:
                    return
                c = RING * i + j
                act.wait_ge(gathered[j], GATH * (i + ITERS + 1))
                act.wait_ge(sh_in[j], 16 * (i + 1))
                wait(act, weights_used, 2 * c - 2)
                for t in range(TILES):
                    act.activation(q[:, j % 2, t, 8:40], g[:, j, t, 0:FEAT], ACT.Copy, scale=sh[:, j, t, 0:1])
                act.activation(q[:, j % 2, :, 40:48], g[:, j, :, 0:MUL], ACT.Copy).then_inc(coefs_ready, 1)

            def after(i, j, n):
                return i + (j + n) // RING, (j + n) % RING

            act.wait_ge(acc_b_clear, 3)
            relu(0, 0, 0)
            relu(0, 0, 1)
            coefs(0, 0)
            relu(0, 1, 0)

            def steps(i):
                for j in range(RING):
                    relu(*after(i, j, 1), 1)
                    coefs(*after(i, j, 1))
                    relu(*after(i, j, 2), 0)

            over_iterations(act, steps)

        @block.tensor
        def _(pe):
            extra = pe.alloc_register("pe_extra")
            pe.reg_mov(extra, 0)

            deg = ps[:, H_BANK, 0:NR]
            pe.wait_ge(zero_ready, 1)
            pe.matmul(deg, zero_b, zero_b[:, 0:NR], start=True, stop=False, skip_group_check=True)

            def count(i):
                for b in range(2):
                    pe.wait_ge(hist_ready, 2 * i + b + 1)
                    for t in range(HB):
                        mm = pe.matmul(deg, oh_p[:, b, :, t], oh_r[:, b, :, t], start=False, stop=False,
                                       skip_group_check=True)
                    mm.then_inc(hist_used, 1)

            with pe.Fori(0, HBATCH // 2) as i:
                count(i)
            pe.matmul(deg, zero_b, zero_b[:, 0:NR], start=False, stop=True,
                      skip_group_check=True).then_inc(degrees_done, 1)

            def segment_sums(oh, lhs, j, b, done, layer):
                groups = [(lhs[0], 0, 0)] if layer == 0 else [(lhs[0], 0, 0), (lhs[1], 128, 1)]
                for rows, col, _ in groups:
                    for t in range(TILES):
                        r = rows(t)
                        m = r.shape[1]
                        mm = pe.matmul(ps[0:m, S_BANK + b, col:col + WIN], r, oh(t),
                                       start=(t == 0), stop=(t == TILES - 1))
                mm.then_inc(done, 1)

            def more_windows(c, lhs, j, b, layer):
                span = pe.value_load(row_i[0:1, 1, bass.ds(c, 1)], min_val=0, max_val=NODES)
                with pe.If(span > WIN - 1):
                    with pe.Fori(WIN, span + 1, WIN):
                        pe.reg_add(extra, extra, 1)
                        pe.wait_ge(x_onehot, pe.snap(extra))
                        segment_sums(lambda t: onehot_x[:, t, :], lhs, j, b, x_seg, layer)

            def take(n, c, j, b, rows):
                lhs = [rows]
                pe.wait_ge(onehot1_ready, n + 1)
                wait(pe, added1, n - 1)
                segment_sums(lambda t: onehot[:, b, t, :], lhs, j, b, seg1_done, 0)
                more_windows(c, lhs, j, b, 0)

            def early_norms(e):
                pe.wait_ge(early_p_ready, e + 1)
                for t in range(TILES):
                    mm = pe.matmul(ps[:, W_BANK + t // 4, NR * (t % 4):NR * (t % 4 + 1)],
                                   early_p[:, P * t:P * (t + 1)], norm_src[:, :], start=True, stop=True)
                mm.then_inc(early_norm_psum, 1)

            def beside_early(i):
                for pos, (is_early, k) in enumerate(UNITS):
                    n = len(UNITS) * i + pos
                    if is_early:
                        pe.wait_ge(early_g_ready, 2 * i + k + 1)
                        take(n, 2 * i + k, 0, pos % 2, lambda t: early_g[:, t, :])
                    else:
                        if UNITS[(pos + 1) % len(UNITS)][0]:
                            early_norms(2 * i + UNITS[pos + 1][1])
                        pe.wait_ge(gathered[k], GATH * (i + (EARLY_ITERS + 1)))
                        take(n, RING * i + (EARLY + k), k, pos % 2, lambda t: g[:, k, t, :])

            def alone(i):
                for j in range(RING):
                    pe.wait_ge(gathered[j], GATH * (i + (EARLY_ITERS + 1)))
                    take(RING * i + (A_UNITS - RING * A_ITERS + j), RING * i + (EARLY + j), j, j % 2,
                         lambda t: g[:, j, t, :])
                    if j == LOOK:
                        next_block(pe, blocks1, final_blocks(pe, RING * i + (EARLY + LOOK)), mid_block)

            blocks1 = counter(pe, "pe_blocks1")

            def mid_block(b):
                pe.wait_ge(mid_go, b + 1)
                for r in range(BR):
                    mm = pe.matmul(mid_ps[:, r, :], by_column(staged1)[:, r, :],
                                   w_l0_s[:, :], start=True, stop=True)
                mm.then_inc(mid_ready, 1)

            pe.wait_ge(acc_a_clear, 1)
            beside_early(0)
            with pe.Fori(1, A_ITERS) as i:
                beside_early(i)
            pe.wait_ge(par_loaded, 16 * N_PARAMS)
            with pe.Fori(A_ITERS, REG_ITERS) as i:
                alone(i)
            other_blocks(pe, blocks1, mid_block)

            pe.wait_ge(table2_ready, BLOCKS)
            for n in range(-(-NR // 4)):
                wait(pe, turned_used, n - 1)
                for r in range(4 * n, min(NR, 4 * n + 4)):
                    k = (r - 4 * n) * P
                    mm = pe.transpose(ps[0:32, S_BANK + n % 2, k:k + P], hn[:, r, :], ident[:, :])
                mm.then_inc(turned, 1)

            def half(i, j, ahead):
                j, h = j + ahead // 2, ahead % 2
                return i + j // RING, j % RING, h

            def beyond(i, j, h):
                return isinstance(i, int) and i >= ITERS

            def hidden(i, j, h):
                if beyond(i, j, h):
                    return
                k = 2 * (RING * i + j) + h
                if h == 0:
                    pe.wait_ge(ef_in[j], 16 * (i + 1))
                wait(pe, hidden_ready, k - 1)
                pe.matmul(ps[0:HID, H_BANK + h, :], w1_s[32 * j:32 * j + 32, :],
                          ef[32 * j:32 * j + 32, 512 * h:512 * h + 512], start=True, stop=True,
                          tile_position=(32 * j, 0)).then_inc(hidden_psum, 1)

            def weights(i, j, h):
                if beyond(i, j, h):
                    return
                k = 2 * (RING * i + j) + h
                pe.wait_ge(hidden_ready, k + 1)
                wait(pe, weights_used, k - 1)
                for t in range(4):
                    mm = pe.matmul(w_ps[h][:, t, :], hid[:, h, P * t:P * t + P], w2_s[:, :], start=True, stop=True)
                mm.then_inc(weights_ready, 1)

            def messages_of(b):
                return [lambda t: prod_a[:, b, t, :], lambda t: msg_b[:, b, t, :]]

            def layer2(i):
                for j in range(RING):
                    c = RING * i + j
                    b = j % 2
                    hidden(*half(i, j, 3))
                    weights(*half(i, j, 2))
                    hidden(*half(i, j, 4))
                    weights(*half(i, j, 3))
                    if not (isinstance(c, int) and c == 0):
                        more_windows(c - 1, messages_of(1 - b), j, 1 - b, 1)
                    pe.wait_ge(messages_ready, c + 1)
                    wait(pe, added2, c - 1)
                    segment_sums(lambda t: onehot[:, b, t, :], messages_of(b), j, b, seg2_done, 1)
                    if j == LOOK:
                        next_block(pe, blocks2, final_blocks(pe, RING * i + (LOOK - 1)), out_block)

            hidden(0, 0, 0)
            hidden(0, 0, 1)
            pe.wait_ge(weights_scaled, 1)
            weights(0, 0, 0)
            hidden(0, 1, 0)
            weights(0, 0, 1)
            pe.wait_ge(turned_used, -(-NR // 4))
            blocks2 = counter(pe, "pe_blocks2")

            def out_block(b):
                pe.wait_ge(fin_go, b + 1)
                for r in range(BR):
                    pe.matmul(fin_ps[:, r, :], by_column(staged2[0])[:, r, :], sel_a_s[:, :],
                              start=True, stop=False)
                    mm = pe.matmul(fin_ps[:, r, :], by_column(staged2[1])[:, r, :], sel_b_s[:, :],
                                   start=False, stop=True)
                mm.then_inc(fin_ready, 1)

            over_iterations(pe, layer2)
            more_windows(CHUNKS - 1, messages_of((CHUNKS - 1) % 2), 0, (CHUNKS - 1) % 2, 1)

            other_blocks(pe, blocks2, out_block)

        @block.vector
        def _(dve):
            extra = dve.alloc_register("dve_extra")
            copied = dve.alloc_register("dve_copied")
            dve.reg_mov(extra, 0)
            dve.reg_mov(copied, 0)
            chain = [0]

            def link(ins):
                chain[0] += 1
                ins.then_inc(dve_chain, 1)
                dve.wait_ge(dve_chain, chain[0])

            def rows(ap, n):
                return ap[:, :, None].to_broadcast([P, NR, n])

            roots = [0]

            def rsqrt(v, y, link=link, number=None):
                if number is None:
                    roots[0] += 1
                    number = roots[0]
                n = v.shape[1]
                dve.sem_inc(root_asked, 1)
                dve.wait_ge(root_given, number)
                t = stat[:, 0, 0:n]
                link(dve.reciprocal(y, root[:, 0:n]))
                link(dve.tensor_tensor(t, y, y, ALU.mult))
                link(dve.tensor_tensor(t, t, v, ALU.mult))
                link(dve.tensor_scalar(t, t, -0.5, 1.5, ALU.mult, ALU.add))
                link(dve.tensor_tensor(y, y, t, ALU.mult))

            def centre(x, xc, hn, link=link, number=None):
                n = x.shape[1]
                total, v = stat[:, 0, 0:n], stat[:, 1, 0:n]
                link(dve.tensor_reduce(total, x, AX, ALU.add))
                link(dve.tensor_scalar(v, total, -1.0 / FEAT, None, ALU.mult))
                link(dve.tensor_tensor(xc, x, v[:, :, None].to_broadcast([P, n, FEAT]), ALU.add))
                link(dve.tensor_tensor(hn, xc, xc, ALU.mult))
                link(dve.tensor_reduce(total, hn, AX, ALU.add))
                link(dve.tensor_scalar(v, total, 1.0 / FEAT, EPS, ALU.mult, ALU.add))
                rsqrt(v, stat[:, 2, 0:n], link, number)

            dve.memset(w2_s[:, :], 0.0).then_inc(params_clear, 1)
            dve.memset(zero_b, 0.0).then_inc(zero_ready, 1)
            link(dve.memset(g[:, :, :, FEAT:FEAT + 1], 1.0))

            dve.wait_ge(iota_done, 2)
            for iota, m in ((iota_p, P), (iota_r, NR)):
                link(dve.tensor_copy(iota, iota_all[:, 0:m, None].to_broadcast([P, m, HB])))

            dve.wait_ge(x_loaded, 16)
            centre(x[:, :, :], xc[:, :, :], hn[:, :, :])

            dve.wait_ge(src_loaded, 16)
            link(dve.tensor_scalar(src_p, src_i, BR_LOG, P - 1, ALU.logical_shift_right, ALU.bitwise_and))
            link(dve.tensor_scalar(src_b, src_i, BLOCK_LOG, BR_LOG, ALU.logical_shift_right,
                                   ALU.logical_shift_left))
            link(dve.scalar_tensor_tensor(out=src_r, in0=src_i, scalar=BR - 1, in1=src_b,
                                          op0=ALU.bitwise_and, op1=ALU.bitwise_or))
            link(dve.tensor_copy(dig_p, src_p))
            link(dve.tensor_copy(dig_r, src_r))

            def count(i):
                for b in range(2):
                    n = 2 * i + b
                    wait(dve, hist_used, n - 1)
                    for iota, dig, oh, m in ((iota_p, dig_p, oh_p, P), (iota_r, dig_r, oh_r, NR)):
                        ins = dve.tensor_tensor(oh[:, b, :, :], iota,
                                                dig[:, None, bass.ds(n * HB, HB)].to_broadcast([P, m, HB]),
                                                ALU.is_equal)
                    ins.then_inc(hist_ready, 1)

            count(0)
            with dve.Fori(1, HBATCH // 2) as i:
                count(i)

            dve.wait_ge(degrees_done, 1)
            link(dve.tensor_scalar(stat[:, 1, :], ps[:, H_BANK, 0:NR], 1.0, None, ALU.max))
            rsqrt(stat[:, 1, :], norm_src[:, :])
            link(dve.tensor_tensor(norm_src[:, :], norm_src[:, :], stat[:, 2, :], ALU.mult))
            dve.scalar_tensor_tensor(out=hn[:, :, :], in0=xc[:, :, :], scalar=0.0, in1=rows(norm_src[:, :], FEAT),
                                     op0=ALU.max, op1=ALU.mult).then_inc(table1_ready, 1)

            dve.wait_ge(dstc_loaded, 16)
            dve.tensor_reduce(mm_c[:, 0, :], dst_c, AX, ALU.min).then_inc(bounds_done, 1)
            dve.tensor_reduce(mm_c[:, 1, :], dst_c, AX, ALU.max).then_inc(bounds_done, 1)
            dve.wait_ge(dst_loaded, 16)
            link(dve.tensor_copy(dst_rel[:, :], dst_i))
            dve.memset(acc_a[:, :], 0.0).then_inc(acc_a_clear, 1)
            link(dve.memset(early_g[:, :, FEAT:FEAT + 1], 1.0))
            dve.wait_ge(bounds_in, 32)
            link(dve.tensor_tensor(dst_rel[:, :].rearrange("p (c t) -> p c t", t=TILES),
                                   dst_rel[:, :].rearrange("p (c t) -> p c t", t=TILES),
                                   bound[:, 0, :, None].to_broadcast([P, CHUNKS, TILES]), ALU.subtract))
            link(dve.tensor_copy(row_i[:, 0, :], bound[0:1, 0, :]))
            link(dve.tensor_tensor(row_i[:, 1, :], bound[0:1, 1, :], bound[0:1, 0, :], ALU.subtract))
            link(dve.memset(later, float(NODES - 1)))
            link(dve.tensor_copy(later[:, 0, 0:CHUNKS - 1], bound[0:1, 0, 1:CHUNKS]))
            shift, k = 1, 0
            while shift < CHUNKS:
                link(dve.tensor_tensor(later[:, 1 - k, 0:CHUNKS], later[:, k, 0:CHUNKS],
                                       later[:, k, shift:shift + CHUNKS], ALU.min))
                shift, k = 2 * shift, 1 - k
            link(dve.tensor_copy(row_i[:, 2, :], later[:, k, 0:CHUNKS]))
            link(dve.tensor_scalar(row_i[:, 2, :], row_i[:, 2, :], BLOCK_LOG, None, ALU.logical_shift_right))
            dve.sem_inc(rows_ready, 1)

            def make_onehot(c, b, done):
                dve.tensor_tensor(onehot[:, b, :, :], iota_all[:, None, 0:WIN].to_broadcast([P, TILES, WIN]),
                                  dst_rel[:, bass.ds(c * TILES, TILES)][:, :, None].to_broadcast([P, TILES, WIN]),
                                  ALU.is_equal).then_inc(done, 1)

            def add_sums(at, b, layer, done):
                if layer == 0:
                    parts = [(acc_a, FEAT + 1, 0)]
                else:
                    parts = [(acc_a, P, 0), (acc_b, MW, 128)]
                for acc, m, col in parts:
                    here = acc[0:m, bass.ds(at, WIN)]
                    ins = dve.tensor_tensor(here, here, ps[0:m, S_BANK + b, col:col + WIN], ALU.add)
                ins.then_inc(done, 1)

            def bounds_of(c):
                return (dve.value_load(row_i[0:1, 0, bass.ds(c, 1)], min_val=0, max_val=NODES - 1),
                        dve.value_load(row_i[0:1, 1, bass.ds(c, 1)], min_val=0, max_val=NODES))

            def more_windows(c, b, base, span, layer):
                with dve.If(span > WIN - 1):
                    dve.reg_add(copied, copied, 1)
                    dve.tensor_copy(dst_x[:, :], dst_rel[:, bass.ds(c * TILES, TILES)]).then_inc(x_copied, 1)
                    with dve.Fori(WIN, span + 1, WIN) as off:
                        dve.wait_ge(x_copied, dve.snap(copied))
                        dve.reg_add(extra, extra, 1)
                        n = dve.snap(extra)
                        dve.tensor_scalar(dst_x[:, :], dst_x[:, :], -float(WIN), None, ALU.add).then_inc(x_shifted, 1)
                        dve.wait_ge(x_shifted, n)
                        dve.tensor_tensor(onehot_x[:, :, :], iota_all[:, None, 0:WIN].to_broadcast([P, TILES, WIN]),
                                          dst_x[:, :, None].to_broadcast([P, TILES, WIN]),
                                          ALU.is_equal).then_inc(x_onehot, 1)
                        dve.wait_ge(x_seg, n)
                        at = nc.s_assert_within(base + off, min_val=0, max_val=NODES - 1)
                        add_sums(at, b, layer, x_added)
                        dve.wait_ge(x_added, n)

            def early_onehots(e):
                dve.wait_ge(early_src_in, 16 * (e + 1))
                dve.tensor_scalar(early_digit, early_src, BR_LOG, P - 1, ALU.logical_shift_right,
                                  ALU.bitwise_and).then_inc(early_digits, 1)
                dve.wait_ge(early_digits, e + 1)
                dve.tensor_scalar(early_p, early_digit, part[:, 0:1], None,
                                  ALU.is_equal).then_inc(early_p_ready, 1)
                dve.tensor_tensor(early_r, iota_all[:, None, 0:NR].to_broadcast([P, TILES, NR]),
                                  dig_r[:, bass.ds(e * TILES, TILES)][:, :, None].to_broadcast([P, TILES, NR]),
                                  ALU.is_equal).then_inc(early_r_ready, 1)
                dve.wait_ge(kept, EARLY)
                dve.tensor_copy(early_x, early[:, bass.ds(e * (TILES * FEAT), TILES * FEAT)].rearrange(
                    "p (t f) -> p t f", f=FEAT)).then_inc(early_chain, 1)
                dve.wait_ge(early_chain, EARLY_LINKS * e + 1)
                dve.tensor_reduce(early_mean, early_x, AX, ALU.add).then_inc(early_chain, 1)
                dve.wait_ge(early_chain, EARLY_LINKS * e + 2)
                dve.tensor_scalar(early_mean, early_mean, -1.0 / FEAT, None, ALU.mult).then_inc(early_chain, 1)
                dve.wait_ge(early_chain, EARLY_LINKS * e + 3)
                dve.tensor_tensor(early_x, early_x, early_mean[:, :, None].to_broadcast([P, TILES, FEAT]),
                                  ALU.add).then_inc(early_chain, 1)

            def early_rows(e):
                dve.wait_ge(early_norm_psum, e + 1)
                dve.wait_ge(early_r_ready, e + 1)
                for b in range(2):
                    half = slice(4 * b, 4 * b + 4)
                    ins = dve.tensor_tensor(early_sel[:, half, :], early_r[:, half, :],
                                            ps[:, W_BANK + b, 0:4 * NR].rearrange("p (t r) -> p t r", r=NR), ALU.mult)
                ins.then_inc(early_chain, 1)
                dve.wait_ge(early_chain, EARLY_LINKS * e + 5)
                dve.tensor_reduce(early_norm, early_sel, AX, ALU.add).then_inc(early_chain, 1)
                dve.wait_ge(early_chain, EARLY_LINKS * e + 6)
                dve.scalar_tensor_tensor(
                    out=early_g[:, :, 0:FEAT],
                    in0=early_x,
                    scalar=0.0, in1=early_norm[:, :, None].to_broadcast([P, TILES, FEAT]),
                    op0=ALU.max, op1=ALU.mult).then_inc(early_g_ready, 1)

            def take(n, c, b):
                base, span = bounds_of(c)
                dve.wait_ge(seg1_done, n + 1)
                wait(dve, added1, n)
                add_sums(base, b, 0, added1)
                more_windows(c, b, base, span, 0)

            def beside_early(i):
                for pos, (is_early, k) in enumerate(UNITS):
                    nxt_i, nxt_pos = (i, pos + 1) if pos + 1 < len(UNITS) else (i + 1, 0)
                    nxt_early, nxt_k = UNITS[nxt_pos]
                    if nxt_early:
                        early_onehots(2 * i + nxt_k)
                    make_onehot(2 * i + nxt_k if nxt_early else RING * nxt_i + (EARLY + nxt_k),
                                1 - pos % 2, onehot1_ready)
                    if is_early:
                        early_rows(2 * i + k)
                    take(len(UNITS) * i + pos, 2 * i + k if is_early else RING * i + (EARLY + k), pos % 2)

            def alone(i):
                for j in range(RING):
                    if not (isinstance(i, int) and j == RING - 1):
                        make_onehot(RING * i + (EARLY + j + 1), 1 - j % 2, onehot1_ready)
                    if j == LOOK:
                        final = final_blocks(dve, RING * i + (EARLY + LOOK))
                    n = RING * i + (A_UNITS - RING * A_ITERS + j)
                    take(n, RING * i + (EARLY + j), j % 2)
                    if j == LOOK:
                        def block_of_sums(b):
                            dve.wait_ge(added1, n + 1)
                            dve.sem_inc(sums_there, 1)
                            mid_block(b)

                        next_block(dve, blocks1, final, block_of_sums)

            early_r_ready, early_chain = sem("early_r_ready"), sem("early_chain")
            blocks1 = counter(dve, "dve_blocks1")

            def mid_block(b):
                step = [0]

                def link(ins):
                    step[0] += 1
                    ins.then_inc(mid_chain, 1)
                    dve.wait_ge(mid_chain, b * MID_LINKS + step[0])

                dve.tensor_copy(staged1, acc_a[0:FEAT + 1, bass.ds(b * BLOCK, BLOCK)]).then_inc(mid_go, 1)
                x_b, hn_b = block_columns(x, b), block_columns(hn, b)
                xc_b, new_x, squares = (xc[:, k * BR:(k + 1) * BR, :] for k in range(3))
                v, y = stat[:, 1, 0:BR], stat[:, 3, 0:BR]
                dve.wait_ge(mid_ready, b + 1)
                link(dve.tensor_scalar(v, mid_ps[:, :, FEAT], 1.0, None, ALU.max))
                rsqrt(v, y, link, 2 * b + 3)
                link(dve.tensor_tensor(xc_b, mid_ps[:, :, 0:FEAT], y[:, :, None].to_broadcast([P, BR, FEAT]), ALU.mult))
                link(dve.tensor_tensor(xc_b, xc_b, b_l0_s[:, None, :].to_broadcast([P, BR, FEAT]), ALU.add))
                dve.scalar_tensor_tensor(out=new_x, in0=xc_b, scalar=0.0, in1=x_b, op0=ALU.max, op1=ALU.add)
                link(dve.scalar_tensor_tensor(out=x_b, in0=xc_b, scalar=0.0, in1=x_b, op0=ALU.max, op1=ALU.add))
                centre(new_x, xc_b, squares, link, 2 * b + 4)
                y = stat[:, 2, 0:BR, None].to_broadcast([P, BR, MUL])
                link(dve.scalar_tensor_tensor(out=hn_b[:, :, 0:MUL], in0=xc_b[:, :, 0:MUL], scalar=0.0, in1=y,
                                              op0=ALU.max, op1=ALU.mult))
                for m in range(3):
                    link(dve.scalar_tensor_tensor(
                        out=hn_b[:, :, MUL + MUL * m:MUL + MUL * m + MUL], in0=xc_b[:, :, MUL + m:FEAT:3],
                        scalar=0.0, in1=y, op0=ALU.max, op1=ALU.mult))
                dve.sem_inc(table2_ready, 1)
                assert step[0] == MID_LINKS, step[0]

            make_onehot(EARLY, 0, onehot1_ready)
            beside_early(0)
            with dve.Fori(1, A_ITERS) as i:
                beside_early(i)
            dve.wait_ge(par_loaded, 16 * N_PARAMS)
            dve.wait_ge(table1_out, 16)
            with dve.Fori(A_ITERS, REG_ITERS - 1) as i:
                alone(i)
            alone(REG_ITERS - 1)
            dve.wait_ge(added1, CHUNKS)
            other_blocks(dve, blocks1, mid_block)
            link(dve.memset(acc_a[:, :], 0.0))
            link(dve.tensor_scalar(w2_s[:, 0:64], w2_s[:, 0:64], float(ALPHA * C110), None, ALU.mult))
            link(dve.tensor_scalar(w2_s[:, 64:256], w2_s[:, 64:256], float(ALPHA), None, ALU.mult))
            dve.tensor_scalar(sel_b_s[64:96, :], sel_b_s[64:96, :], float(SI_SCALE), None,
                              ALU.mult).then_inc(weights_scaled, 1)

            def d_coefs(i, j):
                c = RING * i + j
                b = j % 2
                make_onehot(c, b, onehot2_ready)
                dve.wait_ge(coefs_ready, c + 1)
                dve.tensor_tensor(vsh[:, :, :, :], g[:, j, :, MUL:FEAT].rearrange("p t (m i) -> p t i m", m=3),
                                  sh[:, j, :, None, 1:4].to_broadcast([P, TILES, MUL, 3]),
                                  ALU.mult).then_inc(vsh_ready, 1)
                dve.wait_ge(vsh_ready, c + 1)
                dve.tensor_reduce(q[:, b, :, 0:MUL], vsh[:, :, :, :], AX, ALU.add).then_inc(d_ready, 1)

            onehot2_ready = sem("onehot2_ready")

            def products(c, j, h):
                k = 2 * c + h
                b = j % 2
                w = w_ps[h]
                qt = q[:, b, 4 * h:4 * h + 4, :]
                dve.wait_ge(weights_ready, k + 1)
                dve.tensor_tensor(
                    prod_b[:, h, :, 0:3, :].rearrange("p t m (i o) -> p t m i o", o=MUL),
                    w[:, :, 128:192].rearrange("p t (i o) -> p t i o", o=MUL)[:, :, None, :, :].to_broadcast([P, 4, 3, MUL, MUL]),
                    qt[:, :, 16:40].rearrange("p t (m i) -> p t m i", m=3)[:, :, :, :, None].to_broadcast([P, 4, 3, MUL, MUL]),
                    ALU.mult)
                dve.tensor_tensor(
                    prod_b[:, h, :, 3, :].rearrange("p t (i o) -> p t i o", o=MUL),
                    w[:, :, 192:256].rearrange("p t (i o) -> p t i o", o=MUL),
                    qt[:, :, 40:48, None].to_broadcast([P, 4, MUL, MUL]), ALU.mult).then_inc(prodb_ready, 1)
                if h == 0:
                    dve.wait_ge(d_ready, c + 1)
                dve.tensor_tensor(
                    prod_a[:, b, 4 * h:4 * h + 4, :].rearrange("p t (k o) -> p t k o", o=MUL),
                    w[:, :, 0:128].rearrange("p t (k o) -> p t k o", o=MUL),
                    qt[:, :, 0:16, None].to_broadcast([P, 4, 16, MUL]), ALU.mult).then_inc(weights_used, 1)
                dve.wait_ge(prodb_ready, k + 1)
                dve.tensor_reduce(
                    msg_b[:, b, 4 * h:4 * h + 4, 0:32].rearrange("p t (g o) -> p t g o", o=MUL),
                    prod_b[:, h, :, :, :].rearrange("p t g (i o) -> p t g o i", o=MUL),
                    AX, ALU.add).then_inc(reduced, 1)

            def finish_messages(c, j):
                b = j % 2
                dve.wait_ge(reduced, 2 * c + 2)
                dve.tensor_tensor(
                    msg_b[:, b, :, 32:56].rearrange("p t (m o) -> p t m o", m=3),
                    msg_b[:, b, :, None, 24:32].to_broadcast([P, TILES, 3, MUL]),
                    sh[:, j, :, 1:4, None].to_broadcast([P, TILES, 3, MUL]), ALU.mult).then_inc(messages_ready, 1)

            def join_sums(c, b, base, span):
                dve.wait_ge(seg2_done, c + 1)
                wait(dve, added2, c)
                add_sums(base, b, 1, added2)
                more_windows(c, b, base, span, 1)

            def layer2(i):
                for j in range(RING):
                    c = RING * i + j
                    b = j % 2
                    first = isinstance(c, int) and c == 0
                    if not first:
                        limits = bounds_of(c - 1)
                    products(c, j, 1)
                    if j == LOOK:
                        final = final_blocks(dve, c - 1)
                    if not first:
                        join_sums(c - 1, 1 - b, *limits)
                    finish_messages(c, j)
                    if j == LOOK + 2:
                        next_block(dve, blocks2, final, out_block)
                    if j == LOOK:
                        with dve.If(final > dve.snap(blocks2, min_val=0, max_val=BLOCKS)):
                            dve.wait_ge(added2, c)
                            dve.sem_inc(sums_there, 1)
                            stage(dve.snap(blocks2, min_val=0, max_val=BLOCKS - 1))
                    if not (isinstance(c, int) and c == CHUNKS - 1):
                        nxt = (i, j + 1) if j + 1 < RING else (i + 1, 0)
                        d_coefs(*nxt)
                        products(c + 1, nxt[1], 0)
            blocks2 = counter(dve, "dve_blocks2")

            def stage(b):
                dve.tensor_copy(staged2[0], acc_a[:, bass.ds(b * BLOCK, BLOCK)])
                dve.tensor_copy(staged2[1], acc_b[0:96, bass.ds(b * BLOCK, BLOCK)]).then_inc(fin_go, 1)

            def out_block(b):
                dve.wait_ge(fin_ready, b + 1)
                dve.tensor_tensor(block_columns(xc, b), block_columns(x, b), fin_ps, ALU.add).then_inc(out_ready, 1)

            d_coefs(0, 0)
            products(0, 0, 0)
            dve.wait_ge(turned_used, -(-NR // 4))
            over_iterations(dve, layer2)
            join_sums(CHUNKS - 1, (CHUNKS - 1) % 2, *bounds_of(CHUNKS - 1))
            dve.wait_ge(added2, CHUNKS)

            def last_blocks(b):
                stage(b)
                out_block(b)

            other_blocks(dve, blocks2, last_blocks)


def selections():
    a = np.zeros((P, FEAT), np.float32)
    b = np.zeros((64, FEAT), np.float32)
    for o in range(MUL):
        a[o::MUL, o] = 1.0
        for m in range(3):
            b[m * MUL + o, MUL + 3 * o + m] = 1.0
            b[32 + m * MUL + o, MUL + 3 * o + m] = 1.0
    return a, b


def kernel(x, src, dst, edge_attr_32, edge_attr_4, L0_gnn_weight, L0_gnn_bias, L1_gnn_W1, L1_gnn_b1,
           L1_gnn_W2, L1_gnn_b2, L1_gnn_si_w0, L1_gnn_si_w1):
    import concourse.bacc as bacc
    from concourse.bass_utils import run_bass_kernel_spmd

    edges = CHUNKS * CHUNK
    pad = edges - N_EDGES
    xn = np.pad(np.asarray(x), ((0, NODES - N_NODES), (0, 0)))
    s = np.pad(np.asarray(src), (0, pad), constant_values=NODES - 1)
    d = np.pad(np.asarray(dst), (0, pad), constant_values=N_NODES)
    ea = np.pad(np.asarray(edge_attr_32), ((0, pad), (0, 0))).reshape(CHUNKS, CHUNK, FEAT).transpose(0, 2, 1)
    e4 = np.pad(np.asarray(edge_attr_4), ((0, pad), (0, 0))).reshape(CHUNKS, TILES, P, 4).transpose(0, 2, 1, 3)
    w0 = np.zeros((FEAT + 1, FEAT + 1), np.float32)
    w0[:FEAT, :FEAT] = L0_gnn_weight
    w0[FEAT, FEAT] = 1.0
    mm = MUL * MUL
    w2 = np.concatenate([np.asarray(L1_gnn_W2), np.asarray(L1_gnn_b2)[None, :]])
    w2 = np.concatenate([w2[:, 3 * mm:], w2[:, :mm], w2[:, 2 * mm:3 * mm], w2[:, mm:2 * mm]], axis=1)
    skip = np.zeros((FEAT, FEAT), np.float32)
    skip[:MUL, :MUL] = L1_gnn_si_w0
    for m in range(3):
        skip[MUL + MUL * m:MUL + MUL * m + MUL, MUL + m::3] = L1_gnn_si_w1
    sel_a, sel_b = selections()
    arrays = {
        "x_rows": xn,
        "src_all": s.reshape(CHUNKS * TILES, P).T,
        "src_chunks": s.reshape(CHUNKS, TILES, P).transpose(0, 2, 1),
        "src_rows": s.reshape(CHUNKS, CHUNK),
        "dst_all": d.reshape(CHUNKS * TILES, P).T,
        "dst_chunks": d.reshape(CHUNKS, CHUNK),
        "edge_t": ea,
        "sh_chunks": e4.reshape(CHUNKS, P, TILES * 4),
        "w_l0": w0,
        "b_l0": np.asarray(L0_gnn_bias)[None, :],
        "w1": np.asarray(L1_gnn_W1),
        "b1": np.asarray(L1_gnn_b1)[:, None],
        "w2": w2,
        "skip_w": skip,
        "sel_a": sel_a,
        "sel_b": sel_b,
        "ident_in": np.eye(P, dtype=np.float32),
    }
    arrays = {k: np.ascontiguousarray(v) for k, v in arrays.items()}
    nc = bacc.Bacc("TRN2", target_bir_lowering=False, num_devices=1)
    aps = {k: nc.dram_tensor(k, v.shape, mybir.dt.from_np(v.dtype), kind="ExternalInput").ap()
           for k, v in arrays.items()}
    out = nc.dram_tensor("out", (NODES, FEAT), F32, kind="ExternalOutput").ap()
    gnn_program(nc, **aps, out=out)
    r = run_bass_kernel_spmd(nc, [arrays], core_ids=[0])
    return r.results[0]["out"][:N_NODES]
```
